# Optimizing a Trainium2 kernel written in Bass

```python
import numpy as np
import jax
import jax.numpy as jnp

def _softmax(x, axis=-1):
    return jax.nn.softmax(x, axis=axis)

def _gelu(x):
    return jax.nn.gelu(x, approximate=True)

def _silu(x):
    return jax.nn.silu(x)

def _sigmoid(x):
    return jax.nn.sigmoid(x)

def _layernorm(x, axis=-1, eps=1e-05):
    m = jnp.mean(x, axis=axis, keepdims=True)
    v = jnp.var(x, axis=axis, keepdims=True)
    return (x - m) / jnp.sqrt(v + eps)

def _scatter_add(tgt, idx, src, axis=0):
    return tgt.at[idx].add(src)

def _segment_sum(src, seg, n):
    return jax.ops.segment_sum(src, seg, n)
kernel_name = 'mk_cond_resid_d2_seqx_r4_4a3a72'

def setup_inputs(seed: int=0):
    np.random.seed(seed)
    _w = jnp.asarray

    def _rec_inputs():
        import jax
        import jax.numpy as jnp
        _rk = jax.random.key(seed)
        x = -1.394e-06 + 0.9999 * jax.random.normal(jax.random.fold_in(_rk, 1), (32, 64, 512), jnp.float32)
        _lenS = 64 - jax.random.randint(jax.random.fold_in(_rk, 7), (32,), 0, max(1, 64 // 4) + 1, jnp.int32)
        _lenS2 = 64 - jax.random.randint(jax.random.fold_in(_rk, 8), (32,), 0, max(1, 64 // 4) + 1, jnp.int32)
        cond_2048 = -0.00499425 + 1.0058 * jax.random.normal(jax.random.fold_in(_rk, 11), (32, 512), jnp.float32)
        return (x, cond_2048)
    x, cond_2048 = _rec_inputs()

    def _L0_cond_setup():
        import jax, jax.numpy as jnp
        import numpy as np
        B, T, D = (16, 128, 512)
        key = jax.random.key(seed)
        k0, k1, k2, k3 = jax.random.split(key, 4)
        scale = 1.0 / np.sqrt(D)
        return {'initial_state': jax.random.normal(k0, (B, D), jnp.float32), 'inputs': jax.random.normal(k1, (B, T, D), jnp.float32), 'W_ih': jax.random.normal(k2, (D, 3 * D), jnp.float32) * scale, 'W_hh': jax.random.normal(k3, (D, 3 * D), jnp.float32) * scale, 'b_ih': jnp.zeros((3 * D,), jnp.float32), 'b_hh': jnp.zeros((3 * D,), jnp.float32)}
    _L0_cond_all = _L0_cond_setup()
    _L0_cond_in = {k: v for k, v in _L0_cond_all.items() if k in ('W_ih', 'W_hh', 'b_ih', 'b_hh')}
    del _L0_cond_all

    def _L1_cond_setup():
        import jax, jax.numpy as jnp
        import numpy as np
        NUM_BLOCKS = 8
        NUM_LAYERS = 4
        EPS = 1e-06
        key = jax.random.key(seed)
        ks = jax.random.split(key, 6)
        B, S, H = (4, 1024, 512)
        inputs = jax.random.normal(ks[0], (B, S, H), dtype=jnp.float32)
        query_vectors = jax.random.normal(ks[1], (NUM_LAYERS, H), dtype=jnp.float32) * 0.01
        lim = float(np.sqrt(6.0 / (H + H)))
        Wk = jax.random.uniform(ks[2], (H, H), minval=-lim, maxval=lim, dtype=jnp.float32)
        Wo = jax.random.uniform(ks[3], (H, H), minval=-lim, maxval=lim, dtype=jnp.float32)
        rms_weight = jnp.ones((H,), dtype=jnp.float32)
        ln_gamma = jnp.ones((H,), dtype=jnp.float32)
        ln_beta = jnp.zeros((H,), dtype=jnp.float32)
        return {'inputs': inputs, 'layer_idx': 1, 'rms_weight': rms_weight, 'query_vectors': query_vectors, 'Wk': Wk, 'Wo': Wo, 'ln_gamma': ln_gamma, 'ln_beta': ln_beta}
    _L1_cond_all = _L1_cond_setup()
    _L1_cond_in = {k: v for k, v in _L1_cond_all.items() if k in ('rms_weight', 'Wk', 'Wo', 'ln_gamma', 'ln_beta')}
    del _L1_cond_all
    return {'x': x, 'cond_2048': cond_2048, 'L0_cond_W_ih': _L0_cond_in['W_ih'], 'L0_cond_W_hh': _L0_cond_in['W_hh'], 'L0_cond_b_ih': _L0_cond_in['b_ih'], 'L0_cond_b_hh': _L0_cond_in['b_hh'], 'L1_cond_rms_weight': _L1_cond_in['rms_weight'], 'L1_cond_Wk': _L1_cond_in['Wk'], 'L1_cond_Wo': _L1_cond_in['Wo'], 'L1_cond_ln_gamma': _L1_cond_in['ln_gamma'], 'L1_cond_ln_beta': _L1_cond_in['ln_beta']}

def reference(x, cond_2048, L0_cond_W_ih, L0_cond_W_hh, L0_cond_b_ih, L0_cond_b_hh, L1_cond_rms_weight, L1_cond_Wk, L1_cond_Wo, L1_cond_ln_gamma, L1_cond_ln_beta):
    import jax
    import jax.numpy as jnp

    def _L0_cond_ref(initial_state, inputs, W_ih, W_hh, b_ih, b_hh):
        import jax, jax.numpy as jnp
        import numpy as np
        B, T, D = (16, 128, 512)
        "ScanOverTime(GRU cell): sequential per-timestep module call with\n            dict-state passing; merge_dict_trees stacks the per-step\n            'state_predicted' tensors along axis=1 -> [B, T, D]."

        def cell(h, x):
            gi = x @ W_ih + b_ih
            gh = h @ W_hh + b_hh
            i_r, i_z, i_n = jnp.split(gi, 3, axis=-1)
            h_r, h_z, h_n = jnp.split(gh, 3, axis=-1)
            r = jax.nn.sigmoid(i_r + h_r)
            z = jax.nn.sigmoid(i_z + h_z)
            n = jnp.tanh(i_n + r * h_n)
            h_new = (1.0 - z) * n + z * h
            return (h_new, h_new)
        xs = jnp.swapaxes(inputs, 0, 1)
        _, hs = jax.lax.scan(cell, initial_state, xs)
        return jnp.swapaxes(hs, 0, 1)

    def _L1_cond_ref(inputs, layer_idx, rms_weight, query_vectors, Wk, Wo, ln_gamma, ln_beta):
        import jax, jax.numpy as jnp
        import numpy as np
        NUM_BLOCKS = 8
        NUM_LAYERS = 4
        EPS = 1e-06
        B, S, H = inputs.shape
        block_size = max(1, S // NUM_BLOCKS)
        n_blocks = S // block_size
        block_repr = inputs.reshape(B, n_blocks, block_size, H).sum(axis=2)
        keys = jnp.einsum('bnh,kh->bnk', block_repr, Wk)
        rms = jnp.sqrt(jnp.mean(keys * keys, axis=-1, keepdims=True) + EPS)
        keys = keys / rms * rms_weight
        q = query_vectors[layer_idx]
        scores = jnp.einsum('bnh,h->bn', keys, q)
        attn = jax.nn.softmax(scores, axis=-1)
        attended = jnp.einsum('bn,bnh->bh', attn, block_repr)
        attended = jnp.broadcast_to(attended[:, None, :], (B, S, H))
        proj = jnp.einsum('bsh,kh->bsk', attended, Wo)
        x = inputs + proj
        mu = jnp.mean(x, axis=-1, keepdims=True)
        var = jnp.mean((x - mu) ** 2, axis=-1, keepdims=True)
        out = (x - mu) / jnp.sqrt(var + EPS) * ln_gamma + ln_beta
        return out
    x = x + _L0_cond_ref(cond_2048, x, L0_cond_W_ih, L0_cond_W_hh, L0_cond_b_ih, L0_cond_b_hh)
    x = x + _L1_cond_ref(x, 1, L1_cond_rms_weight, cond_2048, L1_cond_Wk, L1_cond_Wo, L1_cond_ln_gamma, L1_cond_ln_beta)
    return x

_drawn_inputs = setup_inputs


def setup_inputs(seed=0):
    import zlib

    import numpy as np

    out = dict(_drawn_inputs(seed))
    spreads = {'L0_cond_b_ih': (0.0, 0.1),
     'L0_cond_b_hh': (0.0, 0.1),
     'L1_cond_rms_weight': (1.0, 0.2),
     'L1_cond_ln_gamma': (1.0, 0.2),
     'L1_cond_ln_beta': (0.0, 0.1)}
    factors = {}
    for name, (base, spread) in spreads.items():
        noise = np.random.default_rng([zlib.crc32(name.encode()), seed]).standard_normal(out[name].shape)
        drawn = base * np.exp(spread * noise) if base else spread * noise
        out[name] = jnp.asarray(drawn.astype(out[name].dtype))
    for name, factor in factors.items():
        out[name] = (out[name] * factor).astype(out[name].dtype)
    return out
```

```python
from contextlib import ExitStack

import concourse.bass as bass
from concourse import mybir

F32 = mybir.dt.float32
F32R = mybir.dt.float32r
BF16 = mybir.dt.bfloat16
ALU = mybir.AluOpType
ACT = mybir.ActivationFunctionType
AX = mybir.AxisListType

B, T, D = 32, 64, 512
P = 128
NJ = D // P
G3 = 3 * P
Q = P // B
NQ = T // Q
S = 8
NB = T // S
EPS = 1e-6


def gru_block_attention(nc, x, cond, w_ih_d, w_hh_d, b_ih_d, b_hh_d, rms_d, wk_d, wo_d, gamma_d, beta_d, out):
    ctx = ExitStack()
    with ctx:
        def sb(name, shape, dt=F32):
            return ctx.enter_context(nc.sbuf_tensor(name, shape, dt))

        def pb(name):
            return ctx.enter_context(nc.psum_tensor(name, [P, 512], F32))

        def sem(name):
            return ctx.enter_context(nc.semaphore(name))

        w_hh = sb("w_hh", [P, NJ, 3 * D])
        w_ih_hi = sb("w_ih_hi", [P, NJ, 3 * D], F32R)
        w_ih_lo = sb("w_ih_lo", [P, NJ, 3 * D], F32R)
        wk_t = sb("wk_t", [P, NJ, D])
        wo_t = sb("wo_t", [P, NJ, D])
        b_ih = sb("b_ih", [P, 3 * D])
        ident = sb("ident", [P, P])
        same_b = sb("same_b", [P, P])
        own_n = sb("own_n", [P, NJ])
        gamma = sb("gamma", [P, P])
        beta = sb("beta", [P, P])
        wq = sb("wq", [P, D])
        half = sb("half", [P, T])
        bhh_stack = sb("bhh_stack", [P, G3], BF16)
        bhh_pick = sb("bhh_pick", [P, P], BF16)
        x_in = sb("x_in", [P, Q, P])
        xt_hi = sb("xt_hi", [P, NJ, P], F32R)
        xt_lo = sb("xt_lo", [P, NJ, P], F32R)
        gi_tok = sb("gi_tok", [P, 2, G3])
        gi = sb("gi", [P, 2, Q, G3])
        hist = sb("hist", [P, S, P])
        h_t = sb("h_t", [P, P])
        r, z, n = sb("r", [P, P]), sb("z", [P, P]), sb("n", [P, P])
        omz, zh = sb("omz", [P, P]), sb("zh", [P, P])
        x1 = sb("x1", [P, Q, P])
        sums = sb("sums", [P, Q])
        cx = sb("cx", [P, Q, P])
        sq = sb("sq", [P, Q, P])
        bs = sb("bs", [P, 2, P])
        br_cur = sb("br_cur", [P, P])
        xb_all = sb("xb_all", [P, T, P])
        cg_all = sb("cg_all", [P, T, P])
        ssq_all = sb("ssq_all", [P, T])
        br_all = sb("br_all", [P, NB, P])
        br_t = sb("br_t", [P, NJ, NB, B])
        key_ss = sb("key_ss", [P, 2])
        key_dot = sb("key_dot", [P, 2])
        key_rms = sb("key_rms", [P, 2])
        score = sb("score", [P, 2])
        score_n = sb("score_n", [P, 2, NJ])
        neg_max = sb("neg_max", [P, 1])
        probs = sb("probs", [P, NB])
        prob_sum = sb("prob_sum", [P, 1])
        attn = sb("attn", [P, NB])
        proj_sum = sb("proj_sum", [P, 1])
        cp_stat = sb("cp_stat", [P, 2])
        cp_const = sb("cp_const", [P, 1])

        bhh_rows = x1[:].rearrange("p t u -> p (t u)")[:, 0:G3]
        bhh_rest = cx[:].rearrange("p t u -> p (t u)")[:, 0:G3]
        bhh_part = hist[:].rearrange("p s u -> p (s u)")[:, 0:3 * G3 // 2].bitcast(BF16).rearrange(
            "p (g n) -> p g n", g=3)
        q_row = sq[:].rearrange("p t u -> p (t u)")

        end = w_hh[:].rearrange("p k n -> p (k n)")
        prod = end[:, 0:16 * P].rearrange("p (t u) -> p t u", u=P)
        att_w = end[:, 16 * P:24 * P].rearrange("p (n u) -> p n u", u=P)
        keys_sq, keys_wq = end[:, 24 * P:28 * P], end[:, 28 * P:32 * P]
        attended, att_t, proj, scratch = (end[:, c * P:(c + 1) * P] for c in range(32, 36))
        cp = end[:, 36 * P:37 * P]
        pc = end[:, 37 * P:38 * P]
        cross, var_part, var_sum, rstd = (end[:, 38 * P + c * T:38 * P + (c + 1) * T] for c in range(4))

        w_stage = xb_all[:, 0:48, :].rearrange("p t u -> p (t u)").rearrange("p (k n) -> p k n", k=NJ)
        wk_stage = cg_all[:, 0:16, :].rearrange("p t u -> p (t u)").rearrange("p (k n) -> p k n", k=NJ)
        wo_stage = cg_all[:, 16:32, :].rearrange("p t u -> p (t u)").rearrange("p (k n) -> p k n", k=NJ)

        gates_ps, ht_ps, xt_ps = pb("gates_ps"), pb("ht_ps"), pb("xt_ps")
        gi_ps = [pb("gi_ps0"), pb("gi_ps1")]
        small_ps, turn_ps, spare_ps = pb("small_ps"), pb("turn_ps"), pb("spare_ps")

        w_ih_in = [sem(f"w_ih_in{k}") for k in range(NJ)]
        w_hh_in, consts_in, wkwo_in, bhh_in, h0_in = (
            sem("w_hh_in"), sem("consts_in"), sem("wkwo_in"), sem("bhh_in"), sem("h0_in"))
        x_in_ready = sem("x_in_ready")
        x_res_ready = sem("x_res_ready")
        gi_moved = [sem("gi_moved0"), sem("gi_moved1")]
        made = sem("made")
        w_hi_ready, w_lo_ready = sem("w_hi_ready"), sem("w_lo_ready")
        bhh_step, wq_ready = sem("bhh_step"), sem("wq_ready")
        x_turned, x_hi_ready, x_lo_ready = sem("x_turned"), sem("x_hi_ready"), sem("x_lo_ready")
        gi_done, gi_tok_ready = sem("gi_done"), sem("gi_tok_ready")
        w_turned, w_copied = sem("w_turned"), sem("w_copied")
        gates_ready, h_turned, ht_ready = sem("gates_ready"), sem("h_turned"), sem("ht_ready")
        r_pre_ready, z_pre_ready, n_pre_ready = sem("r_pre_ready"), sem("z_pre_ready"), sem("n_pre_ready")
        r_ready, z_ready, n_ready = sem("r_ready"), sem("z_ready"), sem("n_ready")
        rh_ready, zh_ready, on_ready, h_ready = sem("rh_ready"), sem("zh_ready"), sem("on_ready"), sem("h_ready")
        x1_ready, sums_ready, mean_ready, cx_ready = (
            sem("x1_ready"), sem("sums_ready"), sem("mean_ready"), sem("cx_ready"))
        xb_ready, sq_ready, ssq_ready, bs_ready = sem("xb_ready"), sem("sq_ready"), sem("ssq_ready"), sem("bs_ready")
        br_ready, br_saved, br_turned, br_t_ready = (
            sem("br_ready"), sem("br_saved"), sem("br_turned"), sem("br_t_ready"))
        keys_ready, key_sq_ready, key_dot_ready, key_var_ready, key_rms_ready = (
            sem("keys_ready"), sem("key_sq_ready"), sem("key_dot_ready"), sem("key_var_ready"), sem("key_rms_ready"))
        score_ready, scores_ps_ready, max_ready, probs_ready = (
            sem("score_ready"), sem("scores_ps_ready"), sem("max_ready"), sem("probs_ready"))
        att_step, att_turned, att_t_ready, proj_ready = (
            sem("att_step"), sem("att_turned"), sem("att_t_ready"), sem("proj_ready"))
        proj_step, proj_mean_ready, cp_ready, pc_ready, y_ready = (
            sem("proj_step"), sem("proj_mean_ready"), sem("cp_ready"), sem("pc_ready"), sem("y_ready"))
        cp_step, prod_ready, cross_ready, var_part_ready, var_sum_ready, var_ready, rstd_ready = (
            sem("cp_step"), sem("prod_ready"), sem("cross_ready"), sem("var_part_ready"), sem("var_sum_ready"),
            sem("var_ready"), sem("rstd_ready"))
        out_ready, out_stored = sem("out_ready"), sem("out_stored")

        def wait(eng, s, value):
            if not (isinstance(value, int) and value <= 0):
                eng.wait_ge(s, value)

        def quad_of_x(quad):
            return [x[:, bass.ds(quad * Q, Q), j * P:(j + 1) * P] for j in range(NJ)]

        def chunk(w, k, j):
            return w[:, k, :].rearrange("p (g j u) -> p j g u", g=3, j=NJ)[:, j]

        def over_steps(row, steps=Q):
            return row[:, None, :].broadcast_to([P, steps, P])

        block = ctx.enter_context(nc.Block())

        @block.sync
        def _(sp):
            def load_x(tile, ready, quad):
                for j, piece in enumerate(quad_of_x(quad)):
                    sp.dma_start(tile[j * B:(j + 1) * B, :, :], piece).then_inc(ready, 16)

            def move_gi(i, s, before=False):
                idx = s if before else i * S + s + 5
                q, j = (s // Q, s % Q) if before else (i * 2 + (s + 5) // Q, (s + 5) % Q)
                pos = s if before else s + 5
                slot, tok = (pos // Q) % 2, pos % 2
                wait(sp, gi_tok_ready, idx + 1)
                if j == 0 and not (isinstance(q, int) and q < 2):
                    wait(sp, n_pre_ready, (q - 1) * Q)
                for t in range(Q):
                    sp.dma_start(gi[j * B:(j + 1) * B, slot, t, :],
                                 gi_tok[t * B:(t + 1) * B, tok, :]).then_inc(gi_moved[tok], 16)

            def load_ahead(quad):
                wait(sp, x_turned, quad)
                load_x(x_in, x_in_ready, quad)

            def load_residual(quad):
                wait(sp, xb_ready, quad)
                wait(sp, cx_ready, quad)
                wait(sp, bs_ready, quad)
                load_x(x1, x_res_ready, quad)

            def steps(i, last=False):
                for s in range(S):
                    if s % Q == 0 and not last:
                        load_ahead(i * 2 + s // Q + 2)
                    if s % Q == 2:
                        load_residual(i * 2 + s // Q)
                    if not (last and i * S + s + 5 >= T):
                        move_gi(i, s)

            load_x(x_in, x_in_ready, 0)
            for k in range(NJ):
                sp.dma_start(w_stage[:, k, :], w_ih_d[k * P:(k + 1) * P, :]).then_inc(w_ih_in[k], 16)
            for k in range(NJ):
                sp.dma_start(w_hh[:, k, :], w_hh_d[k * P:(k + 1) * P, :]).then_inc(w_hh_in, 16)
            load_ahead(1)
            for stage, w in ((wk_stage, wk_d), (wo_stage, wo_d)):
                sp.dma_start(stage, w.rearrange("(k p) n -> p k n", p=P)).then_inc(wkwo_in, 16)
            for idx in range(5):
                move_gi(0, idx, before=True)
            steps(0)
            with sp.Fori(1, NB - 1) as i:
                steps(i)
            steps(NB - 1, last=True)
            for c in range(NB):
                wait(sp, out_ready, c + 1)
                for j in range(NJ):
                    sp.dma_start(out[:, c * S:(c + 1) * S, j * P:(j + 1) * P],
                                 cg_all[j * B:(j + 1) * B, c * S:(c + 1) * S, :]).then_inc(out_stored, 16)
            wait(sp, out_stored, 16 * NJ * NB)

        @block.gpsimd
        def _(pool):
            pool.memset(ident[:], 0.0).then_inc(made, 1)
            pool.memset(same_b[:], 0.0).then_inc(made, 1)
            pool.memset(bhh_pick[:], 0.0).then_inc(made, 1)
            pool.memset(bhh_stack[:], 0.0).then_inc(made, 1)
            pool.memset(own_n[:], 0.0).then_inc(made, 1)
            pool.wait_ge(made, 5)
            pool.affine_select(out=ident[:], in_=ident[:], compare_op=ALU.not_equal, fill=1.0, base=0,
                               pattern=[[-1, P]], channel_multiplier=1).then_inc(made, 1)
            for g in range(NJ):
                rows = slice(g * B, (g + 1) * B)
                v = same_b[rows, :].rearrange("p (j b) -> p j b", j=NJ)
                pool.wait_ge(made, 6 + 2 * g)
                pool.affine_select(out=v, in_=v, compare_op=ALU.not_equal, fill=1.0, base=0,
                                   pattern=[[0, NJ], [-1, B]], channel_multiplier=1).then_inc(made, 1)
                pool.wait_ge(made, 7 + 2 * g)
                pool.memset(own_n[rows, g:g + 1], 1.0).then_inc(made, 1)
            for g in range(3):
                v = bhh_pick[g * B:g * B + NJ, :].rearrange("p (j b) -> p j b", j=NJ)
                pool.wait_ge(made, 6 + 2 * NJ + g)
                pool.affine_select(out=v, in_=v, compare_op=ALU.not_equal, fill=1.0, base=0,
                                   pattern=[[-1, NJ], [0, B]], channel_multiplier=1).then_inc(made, 1)
            pool.wait_ge(made, 6 + 2 * NJ + 3)
            pool.memset(half[:], -0.5).then_inc(made, 1)

            def quad_work(quad):
                wait(pool, x1_ready, quad + 1)
                pool.tensor_tensor(xb_all[:, bass.ds(quad * Q, Q), :], x1[:], over_steps(beta),
                                   ALU.add).then_inc(xb_ready, 1)
                wait(pool, cx_ready, quad + 1)
                pool.tensor_tensor(cg_all[:, bass.ds(quad * Q, Q), :], cx[:], over_steps(gamma), ALU.mult)
                pool.tensor_tensor(sq[:], cx[:], cx[:], ALU.mult).then_inc(sq_ready, 1)

            def save_block(nb):
                wait(pool, br_ready, nb + 1)
                pool.tensor_copy(br_all[:, bass.ds(nb, 1), :], br_cur[:, None, :]).then_inc(br_saved, 1)

            pool.wait_ge(consts_in, 16 * (3 + 2 * NJ))
            quad_work(0)
            with pool.Fori(1, NB) as i:
                quad_work(i * 2 - 1)
                save_block(i - 1)
                quad_work(i * 2)
            quad_work(NQ - 1)
            save_block(NB - 1)

            pool.wait_ge(key_var_ready, 1)
            pool.tensor_tensor(key_rms[:], key_ss[:], half[:, 0:2], ALU.pow).then_inc(key_rms_ready, 1)
            pool.wait_ge(pc_ready, 1)
            for c in range(NB):
                v = cg_all[:, c * S:(c + 1) * S, :]
                pool.tensor_tensor(v, v, over_steps(pc, S), ALU.add).then_inc(y_ready, 1)
            pool.wait_ge(var_ready, 1)
            pool.tensor_tensor(rstd, var_sum, half[:], ALU.pow).then_inc(rstd_ready, 1)

        @block.scalar
        def _(act):
            act.dma_start(b_ih[:], b_ih_d[None, :].broadcast_to([P, 3 * D])).then_inc(consts_in, 16)
            for part in range(3):
                act.dma_start(bhh_rows[part * B:part * B + NJ, :].rearrange("j (g u) -> j g u", g=3),
                              b_hh_d.rearrange("(g j u) -> j g u", g=3, j=NJ)).then_inc(bhh_in, 16)
            for j in range(NJ):
                act.dma_start(hist[j * B:(j + 1) * B, S - 1, :], cond[:, j * P:(j + 1) * P]).then_inc(h0_in, 16)
            act.dma_start(q_row, cond[1:2, :].broadcast_to([P, D])).then_inc(consts_in, 16)
            act.dma_start(wq[:], rms_d[None, :].broadcast_to([P, D])).then_inc(consts_in, 16)
            for tile, row in ((gamma, gamma_d), (beta, beta_d)):
                for j in range(NJ):
                    act.dma_start(tile[j * B:(j + 1) * B, :],
                                  row[None, j * P:(j + 1) * P].broadcast_to([B, P])).then_inc(consts_in, 16)

            def split_x(quad):
                wait(act, x_turned, quad + 1)
                wait(act, gi_done, quad * Q)
                act.activation(xt_hi[:].rearrange("p k (t b) -> p t k b", t=Q),
                               xt_ps[:].rearrange("p (t k b) -> p t k b", t=Q, k=NJ),
                               ACT.Copy).then_inc(x_hi_ready, 1)

            split_x(0)
            for k in range(NJ):
                act.wait_ge(w_ih_in[k], 16)
                act.activation(w_ih_hi[:, k, :], w_stage[:, k, :], ACT.Copy).then_inc(w_hi_ready, 1)
            split_x(1)
            for c in range(2 * NJ):
                act.wait_ge(w_turned, c + 1)
                act.activation((wk_t if c < NJ else wo_t)[:, c % NJ, :], (turn_ps, spare_ps)[c % 2][:],
                               ACT.Copy).then_inc(w_copied, 1)

            def step(i, s, last=False):
                t = i * S + s
                wait(act, r_pre_ready, t + 1)
                act.activation(r[:], r[:], ACT.Sigmoid).then_inc(r_ready, 1)
                wait(act, z_pre_ready, t + 1)
                act.activation(z[:], z[:], ACT.Sigmoid).then_inc(z_ready, 1)
                wait(act, n_pre_ready, t + 1)
                act.activation(n[:], n[:], ACT.Tanh).then_inc(n_ready, 1)
                if s % Q == 2 and not last:
                    split_x(i * 2 + s // Q + 2)
                if s == 3 and not (isinstance(i, int) and i == 0):
                    save_turned_block(i - 1)

            def save_turned_block(nb):
                wait(act, br_turned, nb + 1)
                act.activation(br_t[:, :, bass.ds(nb, 1), :],
                               turn_ps[:, 0:P].rearrange("p (k n b) -> p k n b", k=NJ, n=1),
                               ACT.Copy).then_inc(br_t_ready, 1)

            for s in range(S):
                step(0, s)
            with act.Fori(1, NB - 1) as i:
                for s in range(S):
                    step(i, s)
            for s in range(S):
                step(NB - 1, s, last=True)
            save_turned_block(NB - 1)
            for half_ in range(2):
                act.wait_ge(keys_ready, half_ + 1)
                wait(act, key_sq_ready, half_)
                act.activation(keys_sq, gi_ps[half_][:], ACT.Square,
                               accum_out=key_ss[:, half_:half_ + 1]).then_inc(key_sq_ready, 1)
            act.wait_ge(max_ready, 1)
            act.activation(probs[:], small_ps[:, 16:16 + NB], ACT.Exp, bias=neg_max[:, 0:1],
                           accum_out=prob_sum[:]).then_inc(probs_ready, 1)

        @block.tensor
        def _(pe):
            def turn_x(quad):
                wait(pe, x_in_ready, (quad + 1) * (16 * NJ))
                wait(pe, x_lo_ready, quad)
                for t in range(Q):
                    mm = pe.transpose(xt_ps[:, t * P:(t + 1) * P], x_in[:, t, :], ident[:])
                mm.then_inc(x_turned, 1)

            def gi_chunk(idx, pos, quad):
                tok, j = pos % 2, pos % Q
                if j == 0:
                    wait(pe, x_lo_ready, quad + 1)
                wait(pe, gi_tok_ready, idx - 1)
                for k in range(NJ):
                    if isinstance(idx, int) and idx == 0:
                        pe.wait_ge(w_lo_ready, k + 1)
                    for a, w in ((xt_hi, w_ih_hi), (xt_hi, w_ih_lo), (xt_lo, w_ih_hi)):
                        mm = pe.matmul(gi_ps[tok][:, 0:G3], a[:, k, :], chunk(w, k, j),
                                       start=(k == 0 and a is xt_hi and w is w_ih_hi),
                                       stop=(k == NJ - 1 and a is xt_lo))
                mm.then_inc(gi_done, 1)

            def add_b_hh(t):
                wait(pe, rh_ready, t)
                pe.matmul(gates_ps[:, 0:G3], bhh_pick[0:3 * B, :], bhh_stack[0:3 * B, :], start=True, stop=False,
                          skip_group_check=True)

            def turn_h(src, t):
                wait(pe, h_ready, t + 1)
                pe.transpose(ht_ps[:, 0:P], src, ident[:]).then_inc(h_turned, 1)

            def turn_block(nb):
                wait(pe, br_ready, nb + 1)
                pe.transpose(turn_ps[:, 0:P], br_cur[:], ident[:]).then_inc(br_turned, 1)

            def quad_mean(quad):
                wait(pe, sums_ready, quad + 1)
                wait(pe, cx_ready, quad)
                pe.matmul(small_ps[:, 0:Q], same_b[:], sums[:], start=True, stop=True).then_inc(mean_ready, 1)

            def step(i, s, first=False, last=False):
                t = i * S + s
                wait(pe, ht_ready, t + 1)
                for k in range(NJ):
                    for j in range(NJ):
                        mm = pe.matmul(gates_ps[j * B:(j + 1) * B, 0:G3], h_t[:, k * B:(k + 1) * B],
                                       chunk(w_hh, k, j), start=False, stop=(k == NJ - 1), skip_group_check=True)
                mm.then_inc(gates_ready, 1)
                if s % Q == 2 and not last:
                    turn_x(i * 2 + s // Q + 2)
                if not (last and t + 5 >= T):
                    gi_chunk(t + 5, s + 5, i * 2 + (s + 5) // Q)
                if s % Q == 0 and not (first and s == 0):
                    quad_mean(i * 2 + s // Q - 1)
                if s == 3 and not first:
                    turn_block(i - 1)
                if not (last and s == S - 1):
                    add_b_hh(t + 1)
                    turn_h(hist[:, s, :], t)

            pe.wait_ge(made, 5 + 1 + 2 * NJ + 3 + 1)
            turn_x(0)
            turn_x(1)
            for idx in range(5):
                gi_chunk(idx, idx, idx // Q)
            pe.wait_ge(bhh_step, 18)
            add_b_hh(0)
            pe.wait_ge(h0_in, 16 * NJ)
            turn_h(hist[:, S - 1, :], -1)
            pe.wait_ge(wkwo_in, 32)
            for c in range(2 * NJ):
                wait(pe, w_copied, c - 1)
                stage = wk_stage if c < NJ else wo_stage
                for k in range(NJ):
                    mm = pe.transpose((turn_ps, spare_ps)[c % 2][:, k * P:(k + 1) * P],
                                      stage[:, k, (c % NJ) * P:(c % NJ + 1) * P], ident[:])
                mm.then_inc(w_turned, 1)
            pe.wait_ge(w_copied, 2 * NJ)
            pe.wait_ge(w_hh_in, 16 * NJ)
            for s in range(S):
                step(0, s, first=True)
            with pe.Fori(1, NB - 1) as i:
                for s in range(S):
                    step(i, s)
            for s in range(S):
                step(NB - 1, s, last=True)

            def keys(half_):
                for k in range(NJ):
                    mm = pe.matmul(gi_ps[half_][:], br_t[:, k, 4 * half_:4 * half_ + 4, :], wk_t[:, k, :],
                                   start=(k == 0), stop=(k == NJ - 1))
                mm.then_inc(keys_ready, 1)

            pe.wait_ge(gi_tok_ready, T)
            keys(0)
            quad_mean(NQ - 1)
            turn_block(NB - 1)
            pe.wait_ge(br_t_ready, NB)
            keys(1)
            pe.wait_ge(score_ready, 1)
            pe.matmul(small_ps[:, 16:16 + NB], same_b[:], score_n[:].rearrange("p h n -> p (h n)"),
                      start=True, stop=True).then_inc(scores_ps_ready, 1)
            pe.wait_ge(att_step, 3)
            pe.transpose(turn_ps[:, 0:P], attended, ident[:]).then_inc(att_turned, 1)
            pe.wait_ge(att_t_ready, 1)
            for k in range(NJ):
                for j in range(NJ):
                    mm = pe.matmul(gates_ps[j * B:(j + 1) * B, 0:P], att_t[:, k * B:(k + 1) * B],
                                   wo_t[:, k, j * P:(j + 1) * P], start=(k == 0), stop=(k == NJ - 1))
            mm.then_inc(proj_ready, 1)
            pe.wait_ge(proj_step, 2)
            pe.matmul(small_ps[:, 32:33], same_b[:], proj_sum[:], start=True, stop=True).then_inc(proj_mean_ready, 1)
            pe.wait_ge(var_part_ready, 2)
            pe.matmul(spare_ps[:, 0:T], same_b[:], var_part, start=True, stop=True).then_inc(var_sum_ready, 1)

        @block.vector
        def _(dve):
            def split_x(quad):
                wait(dve, x_hi_ready, quad + 1)
                hi = xt_hi[:].bitcast(F32).rearrange("p k (t b) -> p t k b", t=Q)
                dve.tensor_tensor(xt_lo[:].rearrange("p k (t b) -> p t k b", t=Q),
                                  xt_ps[:].rearrange("p (t k b) -> p t k b", t=Q, k=NJ), hi,
                                  ALU.subtract).then_inc(x_lo_ready, 1)

            def keep_gi(idx, pos):
                tok, j = pos % 2, pos % Q
                wait(dve, gi_done, idx + 1)
                if not (isinstance(idx, int) and idx < 2):
                    wait(dve, gi_moved[tok], (idx - tok) * (16 * Q // 2))
                dve.tensor_tensor(gi_tok[:, tok, :].rearrange("p (g u) -> p g u", g=3),
                                  gi_ps[tok][:, 0:G3].rearrange("p (g u) -> p g u", g=3),
                                  b_ih[:].rearrange("p (g j u) -> p j g u", g=3, j=NJ)[:, j],
                                  ALU.add).then_inc(gi_tok_ready, 1)

            def copy_h_t(t):
                wait(dve, h_turned, t + 2)
                dve.tensor_copy(h_t[:], ht_ps[:, 0:P]).then_inc(ht_ready, 1)

            def quad_sum(i, slot, quad):
                wait(dve, x_res_ready, (quad + 1) * (16 * NJ))
                wait(dve, xb_ready, quad)
                wait(dve, h_ready, quad * Q + Q)
                dve.tensor_tensor(x1[:], hist[:, Q * slot:Q * slot + Q, :], x1[:], ALU.add
                                  ).then_inc(x1_ready, 1)
                wait(dve, x1_ready, quad + 1)
                dve.tensor_reduce(sums[:], x1[:], AX.X, ALU.add).then_inc(sums_ready, 1)

            def quad_centre(quad):
                wait(dve, mean_ready, quad + 1)
                wait(dve, sq_ready, quad)
                dve.scalar_tensor_tensor(out=cx[:], in0=small_ps[:, 0:Q, None].broadcast_to([P, Q, P]),
                                         scalar=-1.0 / D, in1=x1[:], op0=ALU.mult, op1=ALU.add
                                         ).then_inc(cx_ready, 1)

            def quad_steps_sum(slot):
                dve.tensor_reduce(bs[:, slot, :], x1[:].rearrange("p t u -> p u t"), AX.X, ALU.add
                                  ).then_inc(bs_ready, 1)

            def quad_squares(slot, quad):
                wait(dve, sq_ready, quad + 1)
                dve.tensor_reduce(ssq_all[:, bass.ds(quad * Q, Q)], sq[:], AX.X, ALU.add).then_inc(ssq_ready, 1)

            def block_sum(nb):
                wait(dve, bs_ready, 2 * nb + 2)
                dve.tensor_tensor(br_cur[:], bs[:, 0, :], bs[:, 1, :], ALU.add).then_inc(br_ready, 1)

            def step(i, s, first=False, last=False):
                t = i * S + s
                slot, tt = s // Q, s % Q
                quad = i * 2 + slot
                wait(dve, gates_ready, t + 1)
                if tt == 0:
                    for tok in range(2):
                        wait(dve, gi_moved[tok], (quad + 1) * (2 * 16 * Q))
                dve.tensor_tensor(r[:], gates_ps[:, 0:P], gi[:, slot, tt, 0:P], ALU.add
                                  ).then_inc(r_pre_ready, 1)
                dve.tensor_tensor(z[:], gates_ps[:, P:2 * P], gi[:, slot, tt, P:2 * P], ALU.add
                                  ).then_inc(z_pre_ready, 1)
                wait(dve, r_ready, t + 1)
                dve.tensor_tensor(r[:], gates_ps[:, 2 * P:G3], r[:], ALU.mult).then_inc(rh_ready, 1)
                wait(dve, rh_ready, t + 1)
                dve.tensor_tensor(n[:], r[:], gi[:, slot, tt, 2 * P:G3], ALU.add).then_inc(n_pre_ready, 1)
                wait(dve, z_ready, t + 1)
                dve.tensor_scalar(omz[:], z[:], -1.0, 1.0, ALU.mult, ALU.add)
                dve.tensor_tensor(zh[:], z[:], hist[:, (s - 1) % S, :], ALU.mult).then_inc(zh_ready, 1)
                wait(dve, n_ready, t + 1)
                wait(dve, zh_ready, t + 1)
                dve.tensor_tensor(omz[:], omz[:], n[:], ALU.mult).then_inc(on_ready, 1)
                wait(dve, on_ready, t + 1)
                dve.tensor_tensor(hist[:, s, :], omz[:], zh[:], ALU.add).then_inc(h_ready, 1)
                if last and s == S - 1:
                    return
                copy_h_t(t)
                if not (last and t + 5 >= T):
                    keep_gi(t + 5, s + 5)
                if tt == 2 and not last:
                    split_x(quad + 2)
                if first and s < 3:
                    return
                done = (s + 1) // Q - 1
                dslot, dquad = done % 2, i * 2 + done
                if (s + 1) % Q == 0:
                    quad_sum(i, dslot, dquad)
                if (s + 1) % Q == 1:
                    quad_centre(dquad)
                if (s + 1) % Q == 2:
                    quad_steps_sum(dslot)
                if (s + 1) % Q == 3:
                    quad_squares(dslot, dquad)
                    if dslot == 1:
                        block_sum(i - 1)

            dve.wait_ge(bhh_in, 48)
            dve.wait_ge(made, 5)
            rest = bhh_rows
            done = 0
            for g in range(3):
                for q in range(3):
                    rows = slice(q * B, q * B + NJ)
                    dve.tensor_copy(bhh_part[rows, g, :], rest[rows, :]).then_inc(bhh_step, 1)
                done += 3
                if g < 2:
                    dve.wait_ge(bhh_step, done)
                    for q in range(3):
                        rows = slice(q * B, q * B + NJ)
                        dve.tensor_tensor(bhh_rest[rows, :], rest[rows, :], bhh_part[rows, g, :], ALU.subtract
                                          ).then_inc(bhh_step, 1)
                    done += 3
                    dve.wait_ge(bhh_step, done)
                    rest = bhh_rest
            dve.wait_ge(bhh_step, done)
            for g in range(3):
                rows = slice(g * B, g * B + NJ)
                dve.tensor_copy(bhh_stack[rows, :], bhh_part[rows, g, :]).then_inc(bhh_step, 1)
            split_x(0)
            for k in range(NJ):
                dve.wait_ge(w_hi_ready, k + 1)
                dve.tensor_tensor(w_ih_lo[:, k, :], w_stage[:, k, :], w_ih_hi[:, k, :].bitcast(F32),
                                  ALU.subtract).then_inc(w_lo_ready, 1)
            dve.wait_ge(consts_in, 16 * (3 + 2 * NJ))
            dve.tensor_tensor(wq[:], wq[:], q_row, ALU.mult).then_inc(wq_ready, 1)
            for idx in range(5):
                if idx == Q:
                    split_x(1)
                keep_gi(idx, idx)
            copy_h_t(-1)

            for s in range(S):
                step(0, s, first=True)
            with dve.Fori(1, NB - 1) as i:
                for s in range(S):
                    step(i, s)
            for s in range(S):
                step(NB - 1, s, last=True)

            quad_sum(NB - 1, 1, NQ - 1)
            quad_steps_sum(1)
            block_sum(NB - 1)
            quad_centre(NQ - 1)
            quad_squares(1, NQ - 1)
            dve.wait_ge(wq_ready, 1)
            for half_ in range(2):
                dve.wait_ge(key_sq_ready, half_ + 1)
                wait(dve, key_dot_ready, half_)
                dve.tensor_tensor_reduce(keys_wq, gi_ps[half_][:], wq[:], 1.0, 0.0, ALU.mult, ALU.add,
                                         key_dot[:, half_:half_ + 1]).then_inc(key_dot_ready, 1)
            dve.tensor_scalar(key_ss[:], key_ss[:], 1.0 / D, EPS, ALU.mult, ALU.add).then_inc(key_var_ready, 1)
            dve.wait_ge(key_rms_ready, 1)
            dve.wait_ge(key_dot_ready, 2)
            dve.tensor_tensor(score[:], key_dot[:], key_rms[:], ALU.mult).then_inc(key_dot_ready, 1)
            dve.wait_ge(key_dot_ready, 3)
            dve.tensor_tensor(score_n[:], score[:, :, None].broadcast_to([P, 2, NJ]),
                              own_n[:, None, :].broadcast_to([P, 2, NJ]), ALU.mult).then_inc(score_ready, 1)
            dve.wait_ge(scores_ps_ready, 1)
            dve.tensor_reduce(neg_max[:], small_ps[:, 16:16 + NB], AX.X, ALU.max, negate=True).then_inc(max_ready, 1)
            dve.wait_ge(probs_ready, 1)
            dve.reciprocal(attn[:, 0:1], prob_sum[:]).then_inc(att_step, 1)
            dve.wait_ge(att_step, 1)
            dve.tensor_scalar(probs[:], probs[:], attn[:, 0:1], None, ALU.mult).then_inc(score_ready, 1)
            dve.wait_ge(score_ready, 2)
            dve.wait_ge(br_saved, NB)
            dve.tensor_tensor(att_w, br_all[:], probs[:, :, None].broadcast_to([P, NB, P]), ALU.mult
                              ).then_inc(att_step, 1)
            dve.wait_ge(att_step, 2)
            dve.tensor_reduce(attended, att_w.rearrange("p n u -> p u n"), AX.X, ALU.add
                              ).then_inc(att_step, 1)
            dve.wait_ge(att_turned, 1)
            dve.tensor_copy(att_t, turn_ps[:, 0:P]).then_inc(att_t_ready, 1)
            dve.wait_ge(proj_ready, 1)
            dve.tensor_copy(proj, gates_ps[:, 0:P]).then_inc(proj_step, 1)
            dve.wait_ge(proj_step, 1)
            dve.tensor_reduce(proj_sum[:], proj, AX.X, ALU.add).then_inc(proj_step, 1)
            dve.wait_ge(proj_mean_ready, 1)
            dve.scalar_tensor_tensor(out=cp, in0=small_ps[:, 32:33].broadcast_to([P, P]), scalar=-1.0 / D,
                                     in1=proj, op0=ALU.mult, op1=ALU.add).then_inc(cp_ready, 1)
            dve.wait_ge(cp_ready, 1)
            dve.tensor_tensor(pc, cp, gamma[:], ALU.mult).then_inc(pc_ready, 1)
            dve.tensor_tensor_reduce(scratch, cp, cp, 1.0, 0.0, ALU.mult, ALU.add,
                                     cp_stat[:, 0:1]).then_inc(cp_step, 1)
            dve.wait_ge(cp_step, 1)
            dve.tensor_tensor_reduce(scratch, beta[:], cp, 1.0, 0.0, ALU.mult, ALU.add,
                                     cp_stat[:, 1:2]).then_inc(cp_step, 1)
            dve.wait_ge(cp_step, 2)
            dve.scalar_tensor_tensor(out=cp_const[:], in0=cp_stat[:, 1:2], scalar=-2.0, in1=cp_stat[:, 0:1],
                                     op0=ALU.mult, op1=ALU.add).then_inc(cp_step, 1)
            dve.wait_ge(xb_ready, NQ)
            for c in range(4):
                steps = slice(16 * c, 16 * c + 16)
                dve.wait_ge(cross_ready, c) if c else None
                dve.tensor_tensor(prod, xb_all[:, steps, :], over_steps(cp, 16), ALU.mult
                                  ).then_inc(prod_ready, 1)
                dve.wait_ge(prod_ready, c + 1)
                dve.tensor_reduce(cross[:, steps], prod, AX.X, ALU.add).then_inc(cross_ready, 1)
            dve.wait_ge(cross_ready, 4)
            dve.wait_ge(ssq_ready, NQ)
            dve.scalar_tensor_tensor(out=var_part, in0=cross, scalar=2.0, in1=ssq_all[:],
                                     op0=ALU.mult, op1=ALU.add).then_inc(var_part_ready, 1)
            dve.wait_ge(var_part_ready, 1)
            dve.wait_ge(cp_step, 3)
            dve.tensor_scalar(var_part, var_part, cp_const[:, 0:1], None, ALU.add
                              ).then_inc(var_part_ready, 1)
            dve.wait_ge(var_sum_ready, 1)
            dve.tensor_scalar(var_sum, spare_ps[:, 0:T], 1.0 / D, EPS, ALU.mult, ALU.add).then_inc(var_ready, 1)
            dve.wait_ge(rstd_ready, 1)
            for c in range(NB):
                dve.wait_ge(y_ready, c + 1)
                for t in range(c * S, c * S + S):
                    ins = dve.scalar_tensor_tensor(out=cg_all[:, t, :], in0=cg_all[:, t, :],
                                                   scalar=rstd[:, t:t + 1], in1=xb_all[:, t, :],
                                                   op0=ALU.mult, op1=ALU.add)
                ins.then_inc(out_ready, 1)


_INS = ["x", "cond_2048", "L0_cond_W_ih", "L0_cond_W_hh", "L0_cond_b_ih", "L0_cond_b_hh", "L1_cond_rms_weight",
        "L1_cond_Wk", "L1_cond_Wo", "L1_cond_ln_gamma", "L1_cond_ln_beta"]


def kernel(**inputs):
    import numpy as _np
    import concourse.bacc as _bacc
    from concourse import mybir as _mybir
    from concourse.bass_utils import run_bass_kernel_spmd as _run

    nc = _bacc.Bacc("TRN2", target_bir_lowering=False, num_devices=1)
    arrays, args = {}, []
    for name in _INS:
        a = _np.ascontiguousarray(inputs[name])
        arrays[f"in_{name}_dram"] = a
        args.append(nc.dram_tensor(f"in_{name}_dram", a.shape, _mybir.dt.from_np(a.dtype), kind="ExternalInput").ap())
    args.append(nc.dram_tensor("out_dram", (B, T, D), F32, kind="ExternalOutput").ap())
    gru_block_attention(nc, *args)
    r = _run(nc, [arrays], core_ids=[0])
    return r.results[0]["out_dram"]
```

```python
from contextlib import ExitStack

import concourse.bass as bass
from concourse import mybir

F32 = mybir.dt.float32
F32R = mybir.dt.float32r
BF16 = mybir.dt.bfloat16
ALU = mybir.AluOpType
ACT = mybir.ActivationFunctionType
AX = mybir.AxisListType

B, T, D = 32, 64, 512
P = 128
NJ = D // P
G3 = 3 * P
Q = P // B
NQ = T // Q
S = 8
NB = T // S
EPS = 1e-6


def gru_block_attention(nc, x_rec_d, x_t_d, cond_d, w_ih_d, w_hh_d, b_ih_d, b_hh_d, rms_d, wk_t_d, wo_t_d, gamma_d,
                        beta_d, out):
    ctx = ExitStack()
    with ctx:
        def sb(name, shape, dt=F32):
            return ctx.enter_context(nc.sbuf_tensor(name, shape, dt))

        def pb(name):
            return ctx.enter_context(nc.psum_tensor(name, [P, 512], F32))

        def sem(name):
            return ctx.enter_context(nc.semaphore(name))

        w_hh = sb("w_hh", [P, NJ, 3 * D])
        w_ih_hi = sb("w_ih_hi", [P, NJ, 3 * D], F32R)
        w_ih_lo = sb("w_ih_lo", [P, NJ, 3 * D], F32R)
        wk_t = sb("wk_t", [P, NJ, D])
        wo_t = sb("wo_t", [P, NJ, D])
        b_in = sb("b_in", [P, 3 * D])
        ident = sb("ident", [P, P])
        same_b = sb("same_b", [P, P])
        own_n = sb("own_n", [P, NJ])
        gamma = sb("gamma", [P, P])
        beta = sb("beta", [P, P])
        wq = sb("wq", [P, D])
        half = sb("half", [P, T])
        bhh_stack = sb("bhh_stack", [P, P], BF16)
        bhh_pick = sb("bhh_pick", [P, P], BF16)
        x_t = sb("x_t", [P, NJ, P])
        xt_hi = sb("xt_hi", [P, NJ, P], F32R)
        xt_lo = sb("xt_lo", [P, NJ, P], F32R)
        gi_tok = sb("gi_tok", [P, 2, G3])
        gi = sb("gi", [P, 2, Q * G3])
        hist = sb("hist", [P, S, P])
        h_t = sb("h_t", [P, P])
        r, z, n = sb("r", [P, P]), sb("z", [P, P]), sb("n", [P, P])
        zh = sb("zh", [P, P])
        x1 = sb("x1", [P, Q, P])
        sums = sb("sums", [P, Q])
        cx = sb("cx", [P, Q, P])
        sq = sb("sq", [P, Q, P])
        bs = sb("bs", [P, 2, P])
        br_cur, br_turned = sb("br_cur", [P, P]), sb("br_turned", [P, P])
        xb_all = sb("xb_all", [P, T, P])
        cg_all = sb("cg_all", [P, T, P])
        ssq_all = sb("ssq_all", [P, T])
        br_all = sb("br_all", [P, NB * P])
        br_t = sb("br_t", [P, NJ, NB * B])
        ones = sb("ones", [2, P])
        scalar_warm = sb("scalar_warm", [P, 1])
        key_ss = sb("key_ss", [P, 2])
        key_dot = sb("key_dot", [P, 2])
        key_rms = sb("key_rms", [P, 2])
        score = sb("score", [P, 2])
        score_n = sb("score_n", [P, 2, NJ])
        neg_max = sb("neg_max", [P, 1])
        probs = sb("probs", [P, NB])
        prob_sum = sb("prob_sum", [P, 1])
        attn = sb("attn", [P, NB])
        proj_sum = sb("proj_sum", [P, 1])
        cp_stat = sb("cp_stat", [P, 2])
        cp_const = sb("cp_const", [P, 1])

        bhh_rows, bhh_rest = hist[:, 0, :], hist[:, 1, :]
        bhh_part = hist[:, 2:4, :].rearrange("p s u -> p (s u)").bitcast(BF16).rearrange("p (g n) -> p g n", g=4)
        bias_rows = xb_all[0:2, 48:60, :].rearrange("p t u -> p (t u)")
        q_row = sq[:].rearrange("p t u -> p (t u)")

        end = w_hh[:].rearrange("p k n -> p (k n)")
        prod = end[:, 0:16 * P].rearrange("p (t u) -> p t u", u=P)
        att_w = end[:, 16 * P:24 * P].rearrange("p (n u) -> p n u", u=P)
        keys_sq, keys_wq = end[:, 24 * P:28 * P], end[:, 28 * P:32 * P]
        attended, att_t, proj, scratch = (end[:, c * P:(c + 1) * P] for c in range(32, 36))
        cp = end[:, 36 * P:37 * P]
        pc = end[:, 37 * P:38 * P]
        cross, var_part, var_sum, rstd = (end[:, 38 * P + c * T:38 * P + (c + 1) * T] for c in range(4))

        w_stage = xb_all[:, 0:48, :].rearrange("p t u -> p (t u)").rearrange("p (k n) -> p k n", k=NJ)
        first_tok = cg_all[:, 0:12, :].rearrange("p t u -> p (t u)").rearrange("p (j n) -> p j n", j=NJ)

        gates_ps, keys_ps = pb("gates_ps"), pb("keys_ps")
        gi_ps = [pb("gi_ps0"), pb("gi_ps1")]
        small_ps, third_ps, fourth_ps = pb("small_ps"), pb("third_ps"), pb("fourth_ps")
        bias_ps = [gates_ps, keys_ps, small_ps]
        first_gi_ps = [gi_ps[0], gi_ps[1], third_ps, fourth_ps]

        w_ih_in = [sem(f"w_ih_in{k}") for k in range(NJ)]
        w_hh_in = [sem(f"w_hh_in{k}") for k in range(NJ)]
        bias_in, consts_in, wkwo_in, bhh_in, h0_in = (
            sem("bias_in"), sem("consts_in"), sem("wkwo_in"), sem("bhh_in"), sem("h0_in"))
        x_t_ready = sem("x_t_ready")
        x_res_ready = sem("x_res_ready")
        gi_moved = [sem("gi_moved0"), sem("gi_moved1")]
        warmed, bias_spread = sem("warmed"), sem("bias_spread")
        bias_made, made = sem("bias_made"), sem("made")
        w_hi_ready, w_lo_ready = sem("w_hi_ready"), sem("w_lo_ready")
        bhh_step, b_in_ready, wq_ready = sem("bhh_step"), sem("b_in_ready"), sem("wq_ready")
        x_hi_ready, x_lo_ready = sem("x_hi_ready"), sem("x_lo_ready")
        gi_done, gi_tok_ready = sem("gi_done"), sem("gi_tok_ready")
        gates_ready, ht_ready = sem("gates_ready"), sem("ht_ready")
        z_pre_ready, n_pre_ready = sem("z_pre_ready"), sem("n_pre_ready")
        r_ready, z_ready, n_ready = sem("r_ready"), sem("z_ready"), sem("n_ready")
        rh_ready = sem("rh_ready")
        terms_ready = sem("terms_ready")
        h_ready = sem("h_ready")
        x1_ready, sums_ready, mean_ready, cx_ready = (
            sem("x1_ready"), sem("sums_ready"), sem("mean_ready"), sem("cx_ready"))
        xb_ready, sq_ready, ssq_ready, bs_ready = sem("xb_ready"), sem("sq_ready"), sem("ssq_ready"), sem("bs_ready")
        br_ready, turned_ready, br_saved = sem("br_ready"), sem("turned_ready"), sem("br_saved")
        keys_ready, key_sq_ready, key_dot_ready, key_var_ready, key_rms_ready = (
            sem("keys_ready"), sem("key_sq_ready"), sem("key_dot_ready"), sem("key_var_ready"), sem("key_rms_ready"))
        score_ready, scores_ps_ready, max_ready, probs_ready = (
            sem("score_ready"), sem("scores_ps_ready"), sem("max_ready"), sem("probs_ready"))
        att_step, att_t_ready, proj_ready = sem("att_step"), sem("att_t_ready"), sem("proj_ready")
        proj_step, proj_mean_ready, cp_ready, pc_ready, y_ready = (
            sem("proj_step"), sem("proj_mean_ready"), sem("cp_ready"), sem("pc_ready"), sem("y_ready"))
        cp_step, prod_ready, cross_ready, var_part_ready, var_sum_ready, var_ready, rstd_ready = (
            sem("cp_step"), sem("prod_ready"), sem("cross_ready"), sem("var_part_ready"), sem("var_sum_ready"),
            sem("var_ready"), sem("rstd_ready"))
        out_ready, out_stored = sem("out_ready"), sem("out_stored")

        def wait(eng, s, value):
            if not (isinstance(value, int) and value <= 0):
                eng.wait_ge(s, value)

        def chunk(w, k, j):
            return w[:, k, :].rearrange("p (g j u) -> p j g u", g=3, j=NJ)[:, j]

        def over_steps(row, steps=Q):
            return row[:, None, :].broadcast_to([P, steps, P])

        block = ctx.enter_context(nc.Block())

        @block.sync
        def _(sp):
            def move_gi(i, s, before=False):
                idx = s if before else i * S + s + 5
                q, j = (s // Q, s % Q) if before else (i * 2 + (s + 5) // Q, (s + 5) % Q)
                pos = s if before else s + 5
                slot, tok = (pos // Q) % 2, pos % 2
                wait(sp, gi_tok_ready, idx + 1)
                if j == 0 and not (isinstance(q, int) and q < 2):
                    wait(sp, n_pre_ready, (q - 1) * Q)
                sp.dma_start(gi[j * B:(j + 1) * B, slot, :],
                             first_tok[:, j, :] if before and s < Q else gi_tok[:, tok, :]).then_inc(gi_moved[tok], 16)

            def load_ahead(quad):
                wait(sp, x_lo_ready, quad)
                sp.dma_start(x_t[:], x_t_d[:, bass.ds(quad * NJ, NJ), :]).then_inc(x_t_ready, 16)

            def load_residual(quad):
                wait(sp, xb_ready, quad)
                wait(sp, cx_ready, quad)
                wait(sp, bs_ready, quad)
                sp.dma_start(x1[:], x_rec_d[:, bass.ds(quad * Q, Q), :]).then_inc(x_res_ready, 16)

            def steps(i, last=False):
                for s in range(S):
                    if s % Q == 0 and not last:
                        load_ahead(i * 2 + s // Q + 2)
                    if s % Q == 2:
                        load_residual(i * 2 + s // Q)
                    if not (last and i * S + s + 5 >= T):
                        move_gi(i, s)

            def load_w_ih(k):
                sp.dma_start(w_stage[:, k, :], w_ih_d[k * P:(k + 1) * P, :]).then_inc(w_ih_in[k], 16)

            sp.wait_ge(bias_made, 1)
            sp.dma_start(bias_rows[0:1, :], b_ih_d[None, :]).then_inc(bias_in, 16)
            sp.dma_start(bias_rows[1:2, 0:2 * D], b_hh_d[None, 0:2 * D]).then_inc(bias_in, 16)
            load_ahead(0)
            load_w_ih(0)
            load_w_ih(1)
            for part in range(3):
                sp.dma_start(bhh_rows[part * B:part * B + NJ, :],
                             b_hh_d[2 * D:3 * D].rearrange("(j u) -> j u", j=NJ)).then_inc(bhh_in, 16)
            load_w_ih(2)
            load_w_ih(3)
            load_ahead(1)
            sp.dma_start(hist[:, S - 1, :], cond_d).then_inc(h0_in, 16)
            for k in range(NJ):
                sp.dma_start(w_hh[:, k, :], w_hh_d[k * P:(k + 1) * P, :]).then_inc(w_hh_in[k], 16)
            for idx in range(5):
                move_gi(0, idx, before=True)
            sp.dma_start(q_row.rearrange("p (j u) -> p j u", j=NJ),
                         cond_d.rearrange("(j b) u -> b j u", j=NJ)[1:2].broadcast_to([P, NJ, P])
                         ).then_inc(consts_in, 16)
            sp.dma_start(wq[:], rms_d[None, :].broadcast_to([P, D])).then_inc(consts_in, 16)
            for tile, row in ((gamma, gamma_d), (beta, beta_d)):
                for j in range(NJ):
                    sp.dma_start(tile[j * B:(j + 1) * B, :],
                                 row[None, j * P:(j + 1) * P].broadcast_to([B, P])).then_inc(consts_in, 16)
            for tile, w in ((wk_t, wk_t_d), (wo_t, wo_t_d)):
                sp.dma_start(tile[:], w.rearrange("(k p) n -> p k n", p=P)).then_inc(wkwo_in, 16)
            steps(0)
            with sp.Fori(1, NB - 1) as i:
                steps(i)
            steps(NB - 1, last=True)
            for c in range(NB):
                wait(sp, out_ready, c + 1)
                sp.dma_start(out[:, c * S:(c + 1) * S, :], cg_all[:, c * S:(c + 1) * S, :]).then_inc(out_stored, 16)
            wait(sp, out_stored, 16 * NB)

        @block.gpsimd
        def _(pool):
            pool.memset(bias_rows[:, 2 * D:], 0.0).then_inc(bias_made, 1)
            pool.memset(ones[:], 1.0).then_inc(bias_made, 1)
            pool.memset(ident[:], 0.0).then_inc(made, 1)
            pool.memset(same_b[:], 0.0).then_inc(made, 1)
            pool.memset(bhh_pick[:], 0.0).then_inc(made, 1)
            pool.memset(bhh_stack[:], 0.0).then_inc(made, 1)
            pool.memset(own_n[:], 0.0).then_inc(made, 1)
            pool.memset(half[:], -0.5).then_inc(made, 1)
            pool.wait_ge(made, 6)
            pool.affine_select(out=ident[:], in_=ident[:], compare_op=ALU.not_equal, fill=1.0, base=0,
                               pattern=[[-1, P]], channel_multiplier=1).then_inc(made, 1)
            for g in range(NJ):
                rows = slice(g * B, (g + 1) * B)
                v = same_b[rows, :].rearrange("p (j b) -> p j b", j=NJ)
                pool.wait_ge(made, 7 + 2 * g)
                pool.affine_select(out=v, in_=v, compare_op=ALU.not_equal, fill=1.0, base=0,
                                   pattern=[[0, NJ], [-1, B]], channel_multiplier=1).then_inc(made, 1)
                pool.wait_ge(made, 8 + 2 * g)
                pool.memset(own_n[rows, g:g + 1], 1.0).then_inc(made, 1)
            for g in range(3):
                v = bhh_pick[g * B:g * B + NJ, :].rearrange("p (j b) -> p j b", j=NJ)
                pool.wait_ge(made, 7 + 2 * NJ + g)
                pool.affine_select(out=v, in_=v, compare_op=ALU.not_equal, fill=1.0, base=0,
                                   pattern=[[-1, NJ], [0, B]], channel_multiplier=1).then_inc(made, 1)

            def quad_work(quad):
                wait(pool, x1_ready, quad + 1)
                pool.tensor_tensor(xb_all[:, bass.ds(quad * Q, Q), :], x1[:], over_steps(beta),
                                   ALU.add).then_inc(xb_ready, 1)
                wait(pool, cx_ready, quad + 1)
                pool.tensor_tensor(cg_all[:, bass.ds(quad * Q, Q), :], cx[:], over_steps(gamma), ALU.mult)
                pool.tensor_tensor(sq[:], cx[:], cx[:], ALU.mult).then_inc(sq_ready, 1)

            def save_block(nb):
                wait(pool, turned_ready, nb + 1)
                pool.tensor_copy(br_all[:, bass.ds(nb * P, P)], br_cur[:])
                pool.tensor_copy(br_t[:, :, bass.ds(nb * B, B)],
                                 br_turned[:].rearrange("p (k b) -> p k b", k=NJ)).then_inc(br_saved, 1)

            pool.wait_ge(consts_in, 16 * (2 + 2 * NJ))
            pool.wait_ge(wq_ready, 1)
            quad_work(0)
            with pool.Fori(1, NB) as i:
                quad_work(i * 2 - 1)
                save_block(i - 1)
                quad_work(i * 2)
            quad_work(NQ - 1)
            save_block(NB - 1)

            pool.wait_ge(key_var_ready, 1)
            pool.tensor_tensor(key_rms[:], key_ss[:], half[:, 0:2], ALU.pow).then_inc(key_rms_ready, 1)
            pool.wait_ge(pc_ready, 1)
            for c in range(NB):
                v = cg_all[:, c * S:(c + 1) * S, :]
                pool.tensor_tensor(v, v, over_steps(pc, S), ALU.add).then_inc(y_ready, 1)
            pool.wait_ge(var_ready, 1)
            pool.tensor_tensor(rstd, var_sum, half[:], ALU.pow).then_inc(rstd_ready, 1)

        @block.scalar
        def _(act):
            def split_x(quad):
                wait(act, x_t_ready, (quad + 1) * 16)
                wait(act, gi_done, quad * Q)
                act.activation(xt_hi[:], x_t[:], ACT.Copy).then_inc(x_hi_ready, 1)

            act.wait_ge(bias_made, 2)
            act.activation(scalar_warm[0:2, :], ones[:, 0:1], ACT.Sigmoid).then_inc(warmed, 1)
            split_x(0)
            for k in range(NJ):
                act.wait_ge(w_ih_in[k], 16)
                act.activation(w_ih_hi[:, k, :], w_stage[:, k, :], ACT.Copy).then_inc(w_hi_ready, 1)
                if k == 0:
                    for g in range(3):
                        act.wait_ge(bias_spread, g + 1)
                        act.activation(b_in[:, g * D:(g + 1) * D], bias_ps[g][:], ACT.Copy).then_inc(b_in_ready, 1)
            split_x(1)
            def step(i, s, last=False):
                t = i * S + s
                wait(act, gates_ready, t + 1)
                act.activation(r[:], gates_ps[:, 0:P], ACT.Sigmoid).then_inc(r_ready, 1)
                wait(act, z_pre_ready, t + 1)
                act.activation(z[:], z[:], ACT.Sigmoid).then_inc(z_ready, 1)
                wait(act, n_pre_ready, t + 1)
                act.activation(n[:], n[:], ACT.Tanh).then_inc(n_ready, 1)
                if s % Q == 2 and not last:
                    split_x(i * 2 + s // Q + 2)

            for s in range(S):
                step(0, s)
            with act.Fori(1, NB - 1) as i:
                for s in range(S):
                    step(i, s)
            for s in range(S):
                step(NB - 1, s, last=True)
            for half_ in range(2):
                act.wait_ge(keys_ready, half_ + 1)
                wait(act, key_sq_ready, half_)
                act.activation(keys_sq, gi_ps[half_][:], ACT.Square,
                               accum_out=key_ss[:, half_:half_ + 1]).then_inc(key_sq_ready, 1)
            act.wait_ge(max_ready, 1)
            act.activation(probs[:], small_ps[:, 16:16 + NB], ACT.Exp, bias=neg_max[:, 0:1],
                           accum_out=prob_sum[:]).then_inc(probs_ready, 1)

        @block.tensor
        def _(pe):
            def gi_chunk(idx, pos, quad):
                tok, j = pos % 2, pos % Q
                if j == 0:
                    wait(pe, x_lo_ready, quad + 1)
                wait(pe, gi_tok_ready, idx - 1)
                for k in range(NJ):
                    for a, w in ((xt_hi, w_ih_hi), (xt_hi, w_ih_lo), (xt_lo, w_ih_hi)):
                        mm = pe.matmul(gi_ps[tok][:, 0:G3], a[:, k, :], chunk(w, k, j),
                                       start=(k == 0 and a is xt_hi and w is w_ih_hi),
                                       stop=(k == NJ - 1 and a is xt_lo))
                mm.then_inc(gi_done, 1)

            def open_sums(i, s, t):
                if not (isinstance(t, int) and t == 0):
                    wait(pe, terms_ready, t * 3 - 2)
                pe.matmul(gates_ps[:, 2 * P:G3], bhh_pick[0:3 * B, :], bhh_stack[0:3 * B, :], start=True, stop=False,
                          skip_group_check=True)
                if s % Q == 0:
                    for tok in range(2):
                        wait(pe, gi_moved[tok], (i * 2 + s // Q + 1) * 32)
                pe.matmul(gates_ps[:, 0:P], ident[:], gi[:, (s // Q) % 2, (s % Q) * G3:(s % Q) * G3 + P], start=False, stop=False,
                          skip_group_check=True)

            def quad_mean(quad):
                wait(pe, sums_ready, quad + 1)
                wait(pe, cx_ready, quad)
                pe.matmul(small_ps[:, 0:Q], same_b[:], sums[:], start=True, stop=True).then_inc(mean_ready, 1)

            def step(i, s, first=False, last=False):
                t = i * S + s
                for k in range(NJ):
                    if k < 2:
                        wait(pe, ht_ready, t * 2 + k + 1)
                    if first and s == 0:
                        pe.wait_ge(w_hh_in[k], 16)
                    for j in range(NJ):
                        mm = pe.matmul(gates_ps[j * B:(j + 1) * B, 0:G3], h_t[:, k * B:(k + 1) * B],
                                       chunk(w_hh, k, j), start=False, stop=(k == NJ - 1), skip_group_check=True)
                mm.then_inc(gates_ready, 1)
                if not (last and t + 5 >= T):
                    gi_chunk(t + 5, s + 5, i * 2 + (s + 5) // Q)
                if not (last and s == S - 1):
                    open_sums(i, s + 1, t + 1)
                if s % Q == 0 and not (first and s == 0):
                    quad_mean(i * 2 + s // Q - 1)

            pe.wait_ge(bias_made, 2)
            pe.wait_ge(bias_in, 32)
            for g in range(3):
                pe.matmul(bias_ps[g][:], ones[:], bias_rows[:, g * D:(g + 1) * D], start=True, stop=True
                          ).then_inc(bias_spread, 1)
            pe.wait_ge(x_lo_ready, 1)
            for k in range(NJ):
                pe.wait_ge(w_hi_ready, k + 1)
                for j in range(NJ):
                    for a, w in ((xt_hi, w_ih_hi), (xt_lo, w_ih_hi)):
                        pe.matmul(first_gi_ps[j][:, 0:G3], a[:, k, :], chunk(w, k, j), start=(k == 0 and a is xt_hi),
                                  stop=False)
                pe.wait_ge(w_lo_ready, k + 1)
                for j in range(NJ):
                    mm = pe.matmul(first_gi_ps[j][:, 0:G3], xt_hi[:, k, :], chunk(w_ih_lo, k, j), start=False,
                                   stop=(k == NJ - 1))
                    if k == NJ - 1:
                        mm.then_inc(gi_done, 1)
            pe.wait_ge(made, 6 + 1 + 2 * NJ + 3)
            pe.wait_ge(b_in_ready, 3)
            pe.wait_ge(bhh_step, 18)
            gi_chunk(Q, Q, 1)
            open_sums(0, 0, 0)
            for s in range(S):
                step(0, s, first=True)
            with pe.Fori(1, NB - 1) as i:
                for s in range(S):
                    step(i, s)
            for s in range(S):
                step(NB - 1, s, last=True)

            def keys(half_):
                for k in range(NJ):
                    mm = pe.matmul(gi_ps[half_][:], br_t[:, k, half_ * P:(half_ + 1) * P], wk_t[:, k, :],
                                   start=(k == 0), stop=(k == NJ - 1))
                mm.then_inc(keys_ready, 1)

            pe.wait_ge(gi_tok_ready, T)
            pe.wait_ge(wkwo_in, 32)
            pe.wait_ge(br_saved, NB - 1)
            keys(0)
            quad_mean(NQ - 1)
            pe.wait_ge(br_saved, NB)
            keys(1)
            pe.wait_ge(score_ready, 1)
            pe.matmul(small_ps[:, 16:16 + NB], same_b[:], score_n[:].rearrange("p h n -> p (h n)"),
                      start=True, stop=True).then_inc(scores_ps_ready, 1)
            pe.wait_ge(att_t_ready, 1)
            for k in range(NJ):
                for j in range(NJ):
                    mm = pe.matmul(gates_ps[j * B:(j + 1) * B, 0:P], att_t[:, k * B:(k + 1) * B],
                                   wo_t[:, k, j * P:(j + 1) * P], start=(k == 0), stop=(k == NJ - 1))
            mm.then_inc(proj_ready, 1)
            pe.wait_ge(proj_step, 2)
            pe.matmul(small_ps[:, 32:33], same_b[:], proj_sum[:], start=True, stop=True).then_inc(proj_mean_ready, 1)
            pe.wait_ge(var_part_ready, 2)
            pe.matmul(fourth_ps[:, 0:T], same_b[:], var_part, start=True, stop=True).then_inc(var_sum_ready, 1)

        @block.vector
        def _(dve):
            def split_x(quad):
                wait(dve, x_hi_ready, quad + 1)
                dve.tensor_tensor(xt_lo[:], x_t[:], xt_hi[:].bitcast(F32), ALU.subtract).then_inc(x_lo_ready, 1)

            def keep_gi(idx, pos):
                tok, j = pos % 2, pos % Q
                first = isinstance(idx, int) and idx < Q
                bank, dst = (first_gi_ps[j], first_tok[:, j, :]) if first else (gi_ps[tok], gi_tok[:, tok, :])
                wait(dve, gi_done, idx + 1)
                if not first:
                    wait(dve, gi_moved[tok], (idx - tok) * 8)
                dve.tensor_tensor(dst.rearrange("p (g u) -> p g u", g=3),
                                  bank[:, 0:G3].rearrange("p (g u) -> p g u", g=3),
                                  b_in[:].rearrange("p (g j u) -> p j g u", g=3, j=NJ)[:, j],
                                  ALU.add).then_inc(gi_tok_ready, 1)

            parts = (slice(0, B), slice(B, P))

            def quad_sum(i, slot, quad):
                wait(dve, x_res_ready, (quad + 1) * 16)
                wait(dve, xb_ready, quad)
                wait(dve, h_ready, quad * (2 * Q) + 2 * Q)
                dve.tensor_tensor(x1[:], hist[:, Q * slot:Q * slot + Q, :], x1[:], ALU.add
                                  ).then_inc(x1_ready, 1)
                wait(dve, x1_ready, quad + 1)
                dve.tensor_reduce(sums[:], x1[:], AX.X, ALU.add).then_inc(sums_ready, 1)

            def quad_centre(quad):
                wait(dve, mean_ready, quad + 1)
                wait(dve, sq_ready, quad)
                dve.scalar_tensor_tensor(out=cx[:], in0=small_ps[:, 0:Q, None].broadcast_to([P, Q, P]),
                                         scalar=-1.0 / D, in1=x1[:], op0=ALU.mult, op1=ALU.add
                                         ).then_inc(cx_ready, 1)

            def quad_steps_sum(slot):
                dve.tensor_reduce(bs[:, slot, :], x1[:].rearrange("p t u -> p u t"), AX.X, ALU.add
                                  ).then_inc(bs_ready, 1)

            def quad_squares(slot, quad):
                wait(dve, sq_ready, quad + 1)
                dve.tensor_reduce(ssq_all[:, bass.ds(quad * Q, Q)], sq[:], AX.X, ALU.add).then_inc(ssq_ready, 1)

            def block_sum(nb):
                wait(dve, bs_ready, nb * 2 + 2)
                dve.tensor_tensor(br_cur[:], bs[:, 0, :], bs[:, 1, :], ALU.add).then_inc(br_ready, 1)
                wait(dve, br_ready, nb + 1)
                dve.transpose(br_turned[:], br_cur[:]).then_inc(turned_ready, 1)

            def step(i, s, first=False, last=False):
                t = i * S + s
                slot, tt = s // Q, s % Q
                quad = i * 2 + slot
                wait(dve, r_ready, t + 1)
                dve.tensor_tensor(r[:], gates_ps[:, 2 * P:G3], r[:], ALU.mult).then_inc(rh_ready, 1)
                dve.tensor_tensor(z[:], gates_ps[:, P:2 * P], gi[:, slot, tt * G3 + P:tt * G3 + 2 * P], ALU.add
                                  ).then_inc(z_pre_ready, 1)
                wait(dve, rh_ready, t + 1)
                dve.tensor_tensor(n[:], r[:], gi[:, slot, tt * G3 + 2 * P:(tt + 1) * G3], ALU.add).then_inc(n_pre_ready, 1)
                wait(dve, z_ready, t + 1)
                dve.tensor_tensor(zh[:], z[:], hist[:, (s - 1) % S, :], ALU.mult).then_inc(terms_ready, 1)
                wait(dve, n_ready, t + 1)
                for c in parts:
                    dve.scalar_tensor_tensor(out=n[:, c], in0=z[:, c], scalar=1.0, in1=n[:, c],
                                             op0=ALU.subtract, op1=ALU.mult).then_inc(terms_ready, 1)
                for number, c in enumerate(parts):
                    wait(dve, terms_ready, t * 3 + 2 + number)
                    dve.tensor_tensor(hist[:, s, c], zh[:, c], n[:, c], ALU.subtract).then_inc(h_ready, 1)
                if last and s == S - 1:
                    return
                for number, c in enumerate(parts):
                    wait(dve, h_ready, t * 2 + 1 + number)
                    dve.transpose(h_t[:, c], hist[:, s, c]).then_inc(ht_ready, 1)
                if not (last and t + 5 >= T):
                    keep_gi(t + 5, s + 5)
                if tt == 2 and not last:
                    split_x(quad + 2)
                if first and s < 3:
                    return
                done = (s + 1) // Q - 1
                dslot, dquad = done % 2, i * 2 + done
                if (s + 1) % Q == 0:
                    quad_sum(i, dslot, dquad)
                if (s + 1) % Q == 1:
                    quad_centre(dquad)
                if (s + 1) % Q == 2:
                    quad_steps_sum(dslot)
                if (s + 1) % Q == 3:
                    quad_squares(dslot, dquad)
                    if dslot == 1:
                        block_sum(i - 1)

            split_x(0)
            def split_w(k):
                dve.wait_ge(w_hi_ready, k + 1)
                dve.tensor_tensor(w_ih_lo[:, k, :], w_stage[:, k, :], w_ih_hi[:, k, :].bitcast(F32),
                                  ALU.subtract).then_inc(w_lo_ready, 1)

            def part_bhh(g):
                rest = bhh_rest if g else bhh_rows
                done = 6 * g
                if g == 0:
                    dve.wait_ge(bhh_in, 48)
                else:
                    dve.wait_ge(bhh_step, done)
                for q in range(3):
                    rows = slice(q * B, q * B + NJ)
                    dve.tensor_copy(bhh_part[rows, g, :], rest[rows, :]).then_inc(bhh_step, 1)
                dve.wait_ge(bhh_step, done + 3)
                if g < 2:
                    for q in range(3):
                        rows = slice(q * B, q * B + NJ)
                        dve.tensor_tensor(bhh_rest[rows, :], rest[rows, :], bhh_part[rows, g, :], ALU.subtract
                                          ).then_inc(bhh_step, 1)
                    return
                dve.wait_ge(made, 5)
                for g_ in range(3):
                    rows = slice(g_ * B, g_ * B + NJ)
                    dve.tensor_copy(bhh_stack[rows, :], bhh_part[rows, g_, :]).then_inc(bhh_step, 1)

            split_w(0)
            part_bhh(0)
            split_w(1)
            part_bhh(1)
            split_w(2)
            part_bhh(2)
            split_w(3)
            dve.wait_ge(b_in_ready, 3)
            dve.wait_ge(h0_in, 16)
            for c in parts:
                dve.transpose(h_t[:, c], hist[:, S - 1, c]).then_inc(ht_ready, 1)
            for idx in range(Q):
                keep_gi(idx, idx)
            split_x(1)
            keep_gi(Q, Q)

            for s in range(S):
                step(0, s, first=True)
                if s == 1:
                    dve.wait_ge(consts_in, 16 * (2 + 2 * NJ))
                    dve.tensor_tensor(wq[:], wq[:], q_row, ALU.mult).then_inc(wq_ready, 1)
            with dve.Fori(1, NB - 1) as i:
                for s in range(S):
                    step(i, s)
            for s in range(S):
                step(NB - 1, s, last=True)

            quad_sum(NB - 1, 1, NQ - 1)
            quad_steps_sum(1)
            block_sum(NB - 1)
            quad_centre(NQ - 1)
            quad_squares(1, NQ - 1)
            dve.wait_ge(wq_ready, 1)
            for half_ in range(2):
                dve.wait_ge(key_sq_ready, half_ + 1)
                wait(dve, key_dot_ready, half_)
                dve.tensor_tensor_reduce(keys_wq, gi_ps[half_][:], wq[:], 1.0, 0.0, ALU.mult, ALU.add,
                                         key_dot[:, half_:half_ + 1]).then_inc(key_dot_ready, 1)
            dve.tensor_scalar(key_ss[:], key_ss[:], 1.0 / D, EPS, ALU.mult, ALU.add).then_inc(key_var_ready, 1)
            dve.wait_ge(key_rms_ready, 1)
            dve.wait_ge(key_dot_ready, 2)
            dve.tensor_tensor(score[:], key_dot[:], key_rms[:], ALU.mult).then_inc(key_dot_ready, 1)
            dve.wait_ge(key_dot_ready, 3)
            dve.tensor_tensor(score_n[:], score[:, :, None].broadcast_to([P, 2, NJ]),
                              own_n[:, None, :].broadcast_to([P, 2, NJ]), ALU.mult).then_inc(score_ready, 1)
            dve.wait_ge(scores_ps_ready, 1)
            dve.tensor_reduce(neg_max[:], small_ps[:, 16:16 + NB], AX.X, ALU.max, negate=True).then_inc(max_ready, 1)
            dve.wait_ge(probs_ready, 1)
            dve.reciprocal(attn[:, 0:1], prob_sum[:]).then_inc(att_step, 1)
            dve.wait_ge(att_step, 1)
            dve.tensor_scalar(probs[:], probs[:], attn[:, 0:1], None, ALU.mult).then_inc(score_ready, 1)
            dve.wait_ge(score_ready, 2)
            dve.tensor_tensor(att_w, br_all[:].rearrange("p (n u) -> p n u", u=P), probs[:, :, None].broadcast_to([P, NB, P]), ALU.mult
                              ).then_inc(att_step, 1)
            dve.wait_ge(att_step, 2)
            dve.tensor_reduce(attended, att_w.rearrange("p n u -> p u n"), AX.X, ALU.add
                              ).then_inc(att_step, 1)
            dve.wait_ge(att_step, 3)
            dve.transpose(att_t, attended).then_inc(att_t_ready, 1)
            dve.wait_ge(proj_ready, 1)
            dve.tensor_copy(proj, gates_ps[:, 0:P]).then_inc(proj_step, 1)
            dve.wait_ge(proj_step, 1)
            dve.tensor_reduce(proj_sum[:], proj, AX.X, ALU.add).then_inc(proj_step, 1)
            dve.wait_ge(proj_mean_ready, 1)
            dve.scalar_tensor_tensor(out=cp, in0=small_ps[:, 32:33].broadcast_to([P, P]), scalar=-1.0 / D,
                                     in1=proj, op0=ALU.mult, op1=ALU.add).then_inc(cp_ready, 1)
            dve.wait_ge(cp_ready, 1)
            dve.tensor_tensor(pc, cp, gamma[:], ALU.mult).then_inc(pc_ready, 1)
            dve.tensor_tensor_reduce(scratch, cp, cp, 1.0, 0.0, ALU.mult, ALU.add,
                                     cp_stat[:, 0:1]).then_inc(cp_step, 1)
            dve.wait_ge(cp_step, 1)
            dve.tensor_tensor_reduce(scratch, beta[:], cp, 1.0, 0.0, ALU.mult, ALU.add,
                                     cp_stat[:, 1:2]).then_inc(cp_step, 1)
            dve.wait_ge(cp_step, 2)
            dve.scalar_tensor_tensor(out=cp_const[:], in0=cp_stat[:, 1:2], scalar=-2.0, in1=cp_stat[:, 0:1],
                                     op0=ALU.mult, op1=ALU.add).then_inc(cp_step, 1)
            dve.wait_ge(xb_ready, NQ)
            for c in range(4):
                steps = slice(16 * c, 16 * c + 16)
                dve.wait_ge(cross_ready, c) if c else None
                dve.tensor_tensor(prod, xb_all[:, steps, :], over_steps(cp, 16), ALU.mult
                                  ).then_inc(prod_ready, 1)
                dve.wait_ge(prod_ready, c + 1)
                dve.tensor_reduce(cross[:, steps], prod, AX.X, ALU.add).then_inc(cross_ready, 1)
            dve.wait_ge(cross_ready, 4)
            dve.wait_ge(ssq_ready, NQ)
            dve.scalar_tensor_tensor(out=var_part, in0=cross, scalar=2.0, in1=ssq_all[:],
                                     op0=ALU.mult, op1=ALU.add).then_inc(var_part_ready, 1)
            dve.wait_ge(var_part_ready, 1)
            dve.wait_ge(cp_step, 3)
            dve.tensor_scalar(var_part, var_part, cp_const[:, 0:1], None, ALU.add
                              ).then_inc(var_part_ready, 1)
            dve.wait_ge(var_sum_ready, 1)
            dve.tensor_scalar(var_sum, fourth_ps[:, 0:T], 1.0 / D, EPS, ALU.mult, ALU.add).then_inc(var_ready, 1)
            dve.wait_ge(rstd_ready, 1)
            for c in range(NB):
                dve.wait_ge(y_ready, c + 1)
                for t in range(c * S, c * S + S):
                    ins = dve.scalar_tensor_tensor(out=cg_all[:, t, :], in0=cg_all[:, t, :],
                                                   scalar=rstd[:, t:t + 1], in1=xb_all[:, t, :],
                                                   op0=ALU.mult, op1=ALU.add)
                ins.then_inc(out_ready, 1)


def kernel(**inputs):
    import numpy as _np
    import concourse.bacc as _bacc
    from concourse import mybir as _mybir
    from concourse.bass_utils import run_bass_kernel_spmd as _run

    nc = _bacc.Bacc("TRN2", target_bir_lowering=False, num_devices=1)
    x, cond = inputs["x"], inputs["cond_2048"]
    laid_out = {
        "x_rec": x.reshape(B, T, NJ, P).transpose(2, 0, 1, 3).reshape(P, T, P),
        "x_t": x.reshape(B, NQ, Q, NJ, P).transpose(4, 1, 3, 0, 2).reshape(P, NQ * NJ, P),
        "cond": cond.reshape(B, NJ, P).transpose(1, 0, 2).reshape(P, P),
        "w_ih": inputs["L0_cond_W_ih"], "w_hh": inputs["L0_cond_W_hh"],
        "b_ih": inputs["L0_cond_b_ih"], "b_hh": inputs["L0_cond_b_hh"], "rms_weight": inputs["L1_cond_rms_weight"],
        "wk_t": inputs["L1_cond_Wk"].transpose(1, 0), "wo_t": inputs["L1_cond_Wo"].transpose(1, 0),
        "gamma": inputs["L1_cond_ln_gamma"], "beta": inputs["L1_cond_ln_beta"],
    }
    for name in ("w_hh", "wk_t", "wo_t"):
        w = laid_out[name]
        laid_out[name] = w.reshape(NJ, NJ, B, w.shape[1]).transpose(1, 0, 2, 3).reshape(w.shape)
    arrays, args = {}, []
    for name, a in laid_out.items():
        a = _np.ascontiguousarray(a)
        arrays[f"in_{name}_dram"] = a
        args.append(nc.dram_tensor(f"in_{name}_dram", a.shape, _mybir.dt.from_np(a.dtype), kind="ExternalInput").ap())
    args.append(nc.dram_tensor("out_dram", (P, T, P), F32, kind="ExternalOutput").ap())
    gru_block_attention(nc, *args)
    r = _run(nc, [arrays], core_ids=[0])
    got = r.results[0]["out_dram"].reshape(NJ, B, T, P)
    return _np.ascontiguousarray(got.transpose(1, 2, 0, 3)).reshape(B, T, D)
```

```python
from contextlib import ExitStack

import concourse.bass as bass
from concourse import mybir

F32 = mybir.dt.float32
F32R = mybir.dt.float32r
ALU = mybir.AluOpType
ACT = mybir.ActivationFunctionType
AX = mybir.AxisListType

B, T, D = 32, 64, 512
P = 128
NJ = D // P
G3 = 3 * P
Q = P // B
NQ = T // Q
S = 8
NB = T // S
C = 16
DVE_SHARE = 6
DVE_SQUARES = ((S, S + DVE_SHARE), (0, DVE_SHARE))
EPS = 1e-6


def gru_block_attention(nc, x_rec_d, x_t_d, cond_d, w_ih_d, w_hh_d, b_ih_d, b_hh_d, rms_d, wk_t_d, wo_t_d, gamma_d,
                        beta_d, out):
    ctx = ExitStack()
    with ctx:
        def sb(name, shape, dt=F32):
            return ctx.enter_context(nc.sbuf_tensor(name, shape, dt))

        def pb(name):
            return ctx.enter_context(nc.psum_tensor(name, [P, 512], F32))

        def sem(name):
            return ctx.enter_context(nc.semaphore(name))

        w_hh = sb("w_hh", [P, NJ, 3 * D])
        w_ih_hi = sb("w_ih_hi", [P, NJ, 3 * D], F32R)
        w_ih_lo = sb("w_ih_lo", [P, NJ, 3 * D], F32R)
        wk_t = sb("wk_t", [P, NJ, D])
        wo_t = sb("wo_t", [P, NJ, D])
        b_in = sb("b_in", [P, 3 * D])
        ident = sb("ident", [P, P])
        same_b = sb("same_b", [P, P])
        own_n = sb("own_n", [P, NJ])
        gamma = sb("gamma", [P, P])
        beta = sb("beta", [P, P])
        wq = sb("wq", [P, D])
        wq_rec = sb("wq_rec", [P, P])
        half = sb("half", [P, 2])
        bhh_n = sb("bhh_n", [P, P])
        x_t = sb("x_t", [P, NJ, P])
        xt_hi = sb("xt_hi", [P, NJ, P], F32R)
        xt_lo = sb("xt_lo", [P, NJ, P], F32R)
        gi_tok = sb("gi_tok", [P, 2, G3])
        gi = sb("gi", [P, 2, Q * G3])
        hist = sb("hist", [P, S, P])
        h_t = sb("h_t", [P, P])
        rz, n = sb("rz", [P, 2 * P]), sb("n", [P, P])
        r, z = rz[:, 0:P], rz[:, P:2 * P]
        zh = sb("zh", [P, P])
        x1 = sb("x1", [P, Q, P])
        sums = sb("sums", [P, Q])
        keys_sq, keys_wq = sb("keys_sq", [P, D]), sb("keys_wq", [P, D])
        bs = sb("bs", [P, 2, P])
        h_sum = sb("h_sum", [P, P])
        br_cur, br_turned = sb("br_cur", [P, P]), sb("br_turned", [P, P])
        xb_all = sb("xb_all", [P, T, P])
        cx_all = sb("cx_all", [P, T, P])
        br_all = sb("br_all", [P, NB * P])
        br_t = sb("br_t", [P, NJ, NB * B])
        ones = sb("ones", [2, P])
        scalar_warm = sb("scalar_warm", [P, 1])
        wo_sum = sb("wo_sum", [P, NJ])
        key_ss, key_dot = sb("key_ss", [P, 2]), sb("key_dot", [P, 2])
        key_rms, score = sb("key_rms", [P, 2]), sb("score", [P, 2])
        score_n = sb("score_n", [P, 2, NJ])

        bias_rows = xb_all[0:2, 48:60, :].rearrange("p t u -> p (t u)")
        q_row, q_row_rec = keys_sq[:], keys_wq[:, 0:P]

        end = w_hh[:].rearrange("p k n -> p (k n)")
        att_w = end[:, 0:7 * P].rearrange("p (n u) -> p n u", u=P)
        att_first, att_t = (end[:, c * P:(c + 1) * P] for c in range(7, 9))
        cp = end[:, 10 * P:11 * P]
        squares = end[:, 11 * P:27 * P].rearrange("p (t u) -> p t u", u=P)
        dve_squares = end[:, 27 * P:39 * P].rearrange("p (t u) -> p t u", u=P)
        sumsq, var, dev, rstd, fix = (end[:, 39 * P + c * T:39 * P + (c + 1) * T] for c in range(5))
        small = end[:, 39 * P + 5 * T:]
        last_key = small[:, 0:2]
        last_var, last_rms, neg_max, prob_sum, top_max, denom = (small[:, c:c + 1] for c in range(2, 8))
        top = small[:, 8:10]
        share = small[:, 10:12]
        probs = small[:, 16:16 + NB - 1]

        w_stage = xb_all[:, 0:48, :].rearrange("p t u -> p (t u)").rearrange("p (k n) -> p k n", k=NJ)
        first_tok = cx_all[:, 0:12, :].rearrange("p t u -> p (t u)").rearrange("p (j n) -> p j n", j=NJ)

        gates_ps, keys_ps = pb("gates_ps"), pb("keys_ps")
        gi_ps = [pb("gi_ps0"), pb("gi_ps1")]
        small_ps, third_ps, fourth_ps = pb("small_ps"), pb("third_ps"), pb("fourth_ps")
        bias_ps = [gates_ps, keys_ps, small_ps]
        first_gi_ps = [gi_ps[0], gi_ps[1], third_ps, fourth_ps]

        w_ih_in = [sem(f"w_ih_in{k}") for k in range(NJ)]
        w_hh_in = [sem(f"w_hh_in{k}") for k in range(NJ)]
        bias_in, consts_in, wk_in, wo_in, bhh_in, h0_in = (
            sem("bias_in"), sem("consts_in"), sem("wk_in"), sem("wo_in"), sem("bhh_in"), sem("h0_in"))
        x_t_ready = sem("x_t_ready")
        x_res_ready = sem("x_res_ready")
        gi_first = [sem(f"gi_first{t}") for t in range(Q)]
        gi_moved = [sem("gi_moved0"), sem("gi_moved1")]
        warmed, bias_spread = sem("warmed"), sem("bias_spread")
        bias_made, made = sem("bias_made"), sem("made")
        w_hi_ready, w_lo_ready = sem("w_hi_ready"), sem("w_lo_ready")
        b_in_ready, wq_ready = sem("b_in_ready"), sem("wq_ready")
        x_hi_ready, x_lo_ready = sem("x_hi_ready"), sem("x_lo_ready")
        gi_done, gi_tok_ready = sem("gi_done"), sem("gi_tok_ready")
        gates_ready, ht_ready = sem("gates_ready"), sem("ht_ready")
        seeded = sem("seeded")
        n_pre_ready = [sem("n_pre_ready0"), sem("n_pre_ready1")]
        rz_ready, n_ready = sem("rz_ready"), sem("n_ready")
        rh_ready = sem("rh_ready")
        terms_ready = sem("terms_ready")
        h_ready = sem("h_ready")
        x1_ready, sums_ready, mean_ready, cx_ready = (
            sem("x1_ready"), sem("sums_ready"), sem("mean_ready"), sem("cx_ready"))
        xb_ready, bs_ready = sem("xb_ready"), sem("bs_ready")
        br_ready, turned_ready, br_saved = sem("br_ready"), sem("turned_ready"), sem("br_saved")
        wo_summed, wo_centred, pre_step = sem("wo_summed"), sem("wo_centred"), sem("pre_step")
        keys_ready, key_sq_ready, key_dot_ready, key_var_ready, key_rms_ready = (
            sem("keys_ready"), sem("key_sq_ready"), sem("key_dot_ready"), sem("key_var_ready"), sem("key_rms_ready"))
        last_keys_ready, last_dot_ready, last_sq_ready, last_sums_ready, last_var_ready, last_rms_ready = (
            sem("last_keys_ready"), sem("last_dot_ready"), sem("last_sq_ready"), sem("last_sums_ready"),
            sem("last_var_ready"), sem("last_rms_ready"))
        score_ready, scores_ps_ready, max_ready, probs_ready = (
            sem("score_ready"), sem("scores_ps_ready"), sem("max_ready"), sem("probs_ready"))
        top_step, share_ready, denom_step = sem("top_step"), sem("share_ready"), sem("denom_step")
        att_step, att_t_ready, first_proj_ready, last_proj_ready = (
            sem("att_step"), sem("att_t_ready"), sem("first_proj_ready"), sem("last_proj_ready"))
        cp_step, cp_ready = sem("cp_step"), sem("cp_ready")
        u_dve, u_pool, u_pe = sem("u_dve"), sem("u_pool"), sem("u_pe")
        act_squared, dve_squared = sem("act_squared"), sem("dve_squared")
        var_summed, var_ready, dev_ready, refine_step = (
            sem("var_summed"), sem("var_ready"), sem("dev_ready"), sem("refine_step"))
        scaled, act_scaled, out_pool, out_dve = sem("scaled"), sem("act_scaled"), sem("out_pool"), sem("out_dve")
        out_stored = sem("out_stored")

        def wait(eng, s, value):
            if not (isinstance(value, int) and value <= 0):
                eng.wait_ge(s, value)

        def chunk(w, k, j):
            return w[:, k, :].rearrange("p (g j u) -> p j g u", g=3, j=NJ)[:, j]

        def over_steps(row, steps=Q):
            return row[:, None, :].broadcast_to([P, steps, P])

        u_ps = {2: [gates_ps, third_ps], 3: [gi_ps[0], gi_ps[1], keys_ps, fourth_ps]}

        def u_of(c, t):
            if c == 3 or c == 2 and t < S:
                return u_ps[c][t // Q][:, (t % Q) * P:(t % Q + 1) * P]
            return cx_all[:, c * C + t, :]

        def u_count(c, t):
            if c == 0:
                return u_dve, t // Q + 1
            if c == 3 or c == 2 and t < S:
                return u_pe, (c - 2) * 2 + t // Q + 1
            return u_pool, c + t // S

        block = ctx.enter_context(nc.Block())

        @block.sync
        def _(sp):
            def move_gi(i, s):
                idx, pos = i * S + s + 5, s + 5
                q, j = i * 2 + pos // Q, pos % Q
                slot, tok = (pos // Q) % 2, pos % 2
                wait(sp, gi_tok_ready, idx + 1)
                if j == 0 and not (isinstance(q, int) and q < 2):
                    wait(sp, n_pre_ready[1], (q - 1) * Q)
                sp.dma_start(gi[j * B:(j + 1) * B, slot, :], gi_tok[:, tok, :]).then_inc(gi_moved[tok], 16)

            def move_first_gi(t, j):
                if t == 0:
                    wait(sp, gi_tok_ready, j + 1)
                sp.dma_start(gi[j * B:(j + 1) * B, 0, t * G3:(t + 1) * G3], first_tok[t:P:Q, j, :]
                             ).then_inc(gi_first[t], 16)

            def load_ahead(quad):
                wait(sp, x_lo_ready, quad)
                sp.dma_start(x_t[:], x_t_d[:, bass.ds(quad * NJ, NJ), :]).then_inc(x_t_ready, 16)

            def load_residual(quad):
                wait(sp, xb_ready, quad)
                wait(sp, cx_ready, quad)
                wait(sp, bs_ready, quad)
                sp.dma_start(x1[:], x_rec_d[:, bass.ds(quad * Q, Q), :]).then_inc(x_res_ready, 16)

            def steps(i, first=False, last=False):
                for s in range(S):
                    if first and s == 2:
                        sp.dma_start(wo_t[:], wo_t_d.rearrange("(k p) n -> p k n", p=P)).then_inc(wo_in, 16)
                    if first and s == 5:
                        sp.dma_start(wk_t[:], wk_t_d.rearrange("(k p) n -> p k n", p=P)).then_inc(wk_in, 16)
                    if s % Q == 0 and not last:
                        load_ahead(i * 2 + s // Q + 2)
                    if s % Q == 2:
                        load_residual(i * 2 + s // Q)
                    if not (last and i * S + s + 5 >= T):
                        move_gi(i, s)

            def load_w_ih(k):
                sp.dma_start(w_stage[:, k, :], w_ih_d[k * P:(k + 1) * P, :]).then_inc(w_ih_in[k], 16)

            sp.wait_ge(bias_made, 1)
            sp.dma_start(bias_rows[0:1, :], b_ih_d[None, :]).then_inc(bias_in, 16)
            sp.dma_start(bias_rows[1:2, 0:2 * D], b_hh_d[None, 0:2 * D]).then_inc(bias_in, 16)
            load_ahead(0)
            load_w_ih(0)
            load_w_ih(1)
            sp.dma_start(bhh_n[:], b_hh_d[2 * D:3 * D].rearrange("(j u) -> j u", j=NJ)[:, None, :].broadcast_to(
                [NJ, B, P])).then_inc(bhh_in, 16)
            load_w_ih(2)
            load_w_ih(3)
            load_ahead(1)
            sp.dma_start(hist[:, S - 1, :], cond_d).then_inc(h0_in, 16)
            for k in range(NJ):
                sp.dma_start(w_hh[:, k, :], w_hh_d[k * P:(k + 1) * P, :]).then_inc(w_hh_in[k], 16)
            for t in range(Q):
                for j in range(NJ):
                    move_first_gi(t, j)
                if t == 1:
                    move_gi(0, -1)
            sp.dma_start(q_row.rearrange("p (j u) -> p j u", j=NJ),
                         cond_d.rearrange("(j b) u -> b j u", j=NJ)[1:2].broadcast_to([P, NJ, P])
                         ).then_inc(consts_in, 16)
            sp.dma_start(wq[:], rms_d[None, :].broadcast_to([P, D])).then_inc(consts_in, 16)
            for tile, chunks in ((gamma[:], gamma_d.rearrange("(j u) -> j u", j=NJ)),
                                 (beta[:], beta_d.rearrange("(j u) -> j u", j=NJ)),
                                 (wq_rec[:], rms_d.rearrange("(j u) -> j u", j=NJ)),
                                 (q_row_rec, cond_d.rearrange("(j b) u -> j b u", j=NJ)[:, 1, :])):
                sp.dma_start(tile, chunks[:, None, :].broadcast_to([NJ, B, P])).then_inc(consts_in, 16)
            steps(0, first=True)
            with sp.Fori(1, NB - 1) as i:
                steps(i)
            steps(NB - 1, last=True)

            def store(first, end_):
                sp.dma_start(out[:, first:end_, :], cx_all[:, first:end_, :]).then_inc(out_stored, 16)

            for c in range(NB - 1):
                wait(sp, out_pool, c + 1)
                store(c * S, (c + 1) * S)
            for c in range(2):
                wait(sp, out_dve, c + 1)
                store(T - S + c * Q, T - S + (c + 1) * Q)
            sp.wait_ge(out_stored, 16 * (NB + 1))

        @block.gpsimd
        def _(pool):
            pool.memset(bias_rows[:, 2 * D:], 0.0).then_inc(bias_made, 1)
            pool.memset(ones[:], 1.0).then_inc(bias_made, 1)
            pool.memset(ident[:], 0.0).then_inc(made, 1)
            pool.memset(same_b[:], 0.0).then_inc(made, 1)
            pool.memset(own_n[:], 0.0).then_inc(made, 1)
            pool.memset(half[:], -0.5).then_inc(made, 1)
            pool.memset(key_ss[:], 0.0).then_inc(made, 1)
            pool.memset(key_dot[:], 0.0).then_inc(made, 1)
            pool.wait_ge(made, 6)
            pool.affine_select(out=ident[:], in_=ident[:], compare_op=ALU.not_equal, fill=1.0, base=0,
                               pattern=[[-1, P]], channel_multiplier=1).then_inc(made, 1)
            for g in range(NJ):
                rows = slice(g * B, (g + 1) * B)
                v = same_b[rows, :].rearrange("p (j b) -> p j b", j=NJ)
                pool.wait_ge(made, 7 + 2 * g)
                pool.affine_select(out=v, in_=v, compare_op=ALU.not_equal, fill=1.0, base=0,
                                   pattern=[[0, NJ], [-1, B]], channel_multiplier=1).then_inc(made, 1)
                pool.wait_ge(made, 8 + 2 * g)
                pool.memset(own_n[rows, g:g + 1], 1.0).then_inc(made, 1)

            def quad_work(quad):
                wait(pool, x1_ready, quad + 1)
                pool.tensor_tensor(xb_all[:, bass.ds(quad * Q, Q), :], x1[:], over_steps(beta),
                                   ALU.add).then_inc(xb_ready, 1)

            def save_block(nb):
                wait(pool, turned_ready, nb + 1)
                pool.tensor_copy(br_all[:, bass.ds(nb * P, P)], br_cur[:])
                pool.tensor_copy(br_t[:, :, bass.ds(nb * B, B)],
                                 br_turned[:].rearrange("p (k b) -> p k b", k=NJ)).then_inc(br_saved, 1)

            pool.wait_ge(consts_in, 16 * 6)
            quad_work(0)
            with pool.Fori(1, NB) as i:
                quad_work(i * 2 - 1)
                save_block(i - 1)
                quad_work(i * 2)

            pool.wait_ge(key_var_ready, 1)
            pool.tensor_tensor(key_rms[:], key_ss[:], half[:], ALU.pow).then_inc(key_rms_ready, 1)
            quad_work(NQ - 1)
            pool.wait_ge(last_var_ready, 1)
            pool.tensor_tensor(last_rms, last_var, half[:, 0:1], ALU.pow).then_inc(last_rms_ready, 1)
            pool.wait_ge(cp_ready, 1)
            for c in (2, 3, 5):
                v = cx_all[:, c * S:(c + 1) * S, :]
                pool.tensor_tensor(v, v, over_steps(cp, S), ALU.add).then_inc(u_pool, 1)
            for c in range(NB - 1):
                pool.wait_ge(scaled, c + 1)
                v = cx_all[:, c * S:(c + 1) * S, :]
                pool.tensor_tensor(v, v, xb_all[:, c * S:(c + 1) * S, :], ALU.add).then_inc(out_pool, 1)

        @block.scalar
        def _(act):
            def split_x(quad):
                wait(act, x_t_ready, (quad + 1) * 16)
                wait(act, gi_done, quad * Q)
                act.activation(xt_hi[:], x_t[:], ACT.Copy).then_inc(x_hi_ready, 1)

            act.wait_ge(bias_made, 2)
            act.activation(scalar_warm[0:2, :], ones[:, 0:1], ACT.Sigmoid).then_inc(warmed, 1)
            split_x(0)
            for k in range(NJ):
                act.wait_ge(w_ih_in[k], 16)
                act.activation(w_ih_hi[:, k, :], w_stage[:, k, :], ACT.Copy).then_inc(w_hi_ready, 1)
                if k == 0:
                    for g in range(3):
                        act.wait_ge(bias_spread, g + 1)
                        act.activation(b_in[:, g * D:(g + 1) * D], bias_ps[g][:], ACT.Copy).then_inc(b_in_ready, 1)
            split_x(1)
            act.wait_ge(bhh_in, 16)

            def seed_n():
                act.activation(gates_ps[:, 2 * P:G3], bhh_n[:], ACT.Copy).then_inc(seeded, 1)

            def seed_rz(i, s, t):
                if isinstance(t, int) and t < Q:
                    wait(act, gi_first[t], NJ * 16)
                elif s % Q == 0:
                    for tok in range(2):
                        wait(act, gi_moved[tok], (i * 2 + s // Q) * 32)
                first = (s % Q) * G3
                act.activation(gates_ps[:, 0:2 * P], gi[:, (s // Q) % 2, first:first + 2 * P], ACT.Copy
                               ).then_inc(seeded, 1)

            def square_keys(group):
                rows = slice(0, (4 - group) * B)
                act.wait_ge(keys_ready, group + 1)
                act.activation(keys_sq[rows, :], gi_ps[group][rows, :], ACT.Square,
                               accum_out=key_ss[rows, group:group + 1]).then_inc(key_sq_ready, 1)

            def step(i, s, last=False):
                t = i * S + s
                wait(act, gates_ready, t + 1)
                act.activation(rz[:], gates_ps[:, 0:2 * P], ACT.Sigmoid).then_inc(rz_ready, 1)
                if not (last and s == S - 1):
                    wait(act, rh_ready, t + 1)
                    seed_n()
                for number, c in enumerate((slice(0, B), slice(B, P))):
                    wait(act, n_pre_ready[number], t + 1)
                    act.activation(n[:, c], n[:, c], ACT.Tanh).then_inc(n_ready, 1)
                if not (last and s == S - 1):
                    seed_rz(i, s + 1, t + 1)
                if s % Q == 2 and not last:
                    split_x(i * 2 + s // Q + 2)
                if last and s in (4, 6):
                    square_keys(s // 2 - 2)

            seed_n()
            seed_rz(0, 0, 0)
            for s in range(S):
                step(0, s)
            with act.Fori(1, NB - 1) as i:
                for s in range(S):
                    step(i, s)
            for s in range(S):
                step(NB - 1, s, last=True)
            act.wait_ge(max_ready, 1)
            act.activation(probs, fourth_ps[:, 0:NB - 1], ACT.Exp, bias=neg_max[:, 0:1],
                           accum_out=prob_sum).then_inc(probs_ready, 1)
            act.wait_ge(x1_ready, NQ)
            for t in range(Q):
                ins = act.activation(keys_sq[:, t * P:(t + 1) * P], x1[:, t, :], ACT.Copy, accum_out=sums[:, t:t + 1])
            ins.then_inc(sums_ready, 1)
            act.wait_ge(last_dot_ready, 1)
            act.wait_ge(sums_ready, NQ)
            act.activation(keys_sq[:, 0:P], keys_ps[:, 0:P], ACT.Square, accum_out=last_key[:, 0:1]
                           ).then_inc(last_sq_ready, 1)
            act.wait_ge(top_step, 4)
            act.activation(share, top, ACT.Exp).then_inc(share_ready, 1)
            act.wait_ge(share_ready, 1)
            act.activation(scalar_warm[:], prob_sum, ACT.Sqrt).then_inc(warmed, 1)

            def square(c, first, end_):
                for t in range(first, end_):
                    if t == first or t % Q == 0:
                        act.wait_ge(*u_count(c, t))
                    if c and t == first:
                        act.wait_ge(act_squared, c)
                    ins = act.activation(squares[:, t, :], u_of(c, t), ACT.Square,
                                         accum_out=sumsq[:, c * C + t:c * C + t + 1])
                if end_ == C:
                    ins.then_inc(act_squared, 1)

            def deviation(c):
                act.wait_ge(var_ready, c + 1)
                act.activation(dev[:, c * C:(c + 1) * C], var[:, c * C:(c + 1) * C], ACT.Sqrt).then_inc(dev_ready, 1)

            def divide(c, first, end_):
                act.wait_ge(refine_step, 5 * c + 5)
                for t in range(first, end_):
                    ins = act.activation(cx_all[:, c * C + t, :], u_of(c, t), ACT.Identity,
                                         scale=rstd[:, c * C + t:c * C + t + 1])
                    if t % Q == Q - 1:
                        ins.then_inc(act_scaled, 1)

            square(0, 0, DVE_SQUARES[0][0])
            square(0, DVE_SQUARES[0][1], C)
            square(1, DVE_SQUARES[1][1], S)
            deviation(0)
            square(1, S, C)
            square(2, 0, 4)
            deviation(1)
            square(2, 4, C)
            square(3, 0, 4)
            deviation(2)
            square(3, 4, C)
            divide(2, S, S + Q)
            deviation(3)
            divide(2, S + Q, C)
            divide(3, S, C)

        @block.tensor
        def _(pe):
            def gi_chunk(idx, pos, quad):
                tok, j = pos % 2, pos % Q
                if j == 0:
                    wait(pe, x_lo_ready, quad + 1)
                wait(pe, gi_tok_ready, idx - 1)
                for k in range(NJ):
                    for a, w in ((xt_hi, w_ih_hi), (xt_hi, w_ih_lo), (xt_lo, w_ih_hi)):
                        mm = pe.matmul(gi_ps[tok][:, 0:G3], a[:, k, :], chunk(w, k, j),
                                       start=(k == 0 and a is xt_hi and w is w_ih_hi),
                                       stop=(k == NJ - 1 and a is xt_lo))
                mm.then_inc(gi_done, 1)

            def keys(group, part):
                if part == 0:
                    pe.wait_ge(gi_tok_ready, T - 1 + group)
                    pe.wait_ge(wk_in, 16)
                    pe.wait_ge(br_saved, (4, NB - 1)[group])
                rows = slice(0, (4 - group) * B)
                for k in range(part * 2, part * 2 + 2):
                    mm = pe.matmul(gi_ps[group][rows, :], br_t[:, k, group * P:group * P + (4 - group) * B],
                                   wk_t[:, k, :], start=(k == 0), stop=(k == NJ - 1))
                if part == 1:
                    mm.then_inc(keys_ready, 1)

            def quad_mean(quad):
                wait(pe, sums_ready, quad + 1)
                wait(pe, cx_ready, quad)
                pe.matmul(small_ps[:, 0:Q], same_b[:], sums[:], start=True, stop=True).then_inc(mean_ready, 1)

            def step(i, s, first=False, last=False):
                t = i * S + s
                wait(pe, seeded, t * 2 + 2)
                for k in range(NJ):
                    if k < 3:
                        wait(pe, ht_ready, t * 3 + k + 1)
                    if first and s == 0:
                        pe.wait_ge(w_hh_in[k], 16)
                    for j in range(NJ):
                        mm = pe.matmul(gates_ps[j * B:(j + 1) * B, 0:G3], h_t[:, k * B:(k + 1) * B],
                                       chunk(w_hh, k, j), start=False, stop=(k == NJ - 1), skip_group_check=True)
                mm.then_inc(gates_ready, 1)
                if not (last and t + 5 >= T):
                    gi_chunk(t + 5, s + 5, i * 2 + (s + 5) // Q)
                if last and 3 <= s < S - 1:
                    keys((s - 3) // 2, (s - 3) % 2)
                if s % Q == 0 and not (first and s == 0):
                    quad_mean(i * 2 + s // Q - 1)

            pe.wait_ge(bias_made, 2)
            pe.wait_ge(bias_in, 32)
            for g in range(3):
                pe.matmul(bias_ps[g][:], ones[:], bias_rows[:, g * D:(g + 1) * D], start=True, stop=True
                          ).then_inc(bias_spread, 1)
            pe.wait_ge(x_lo_ready, 1)
            for k in range(NJ):
                pe.wait_ge(w_hi_ready, k + 1)
                for j in range(NJ):
                    for a, w in ((xt_hi, w_ih_hi), (xt_lo, w_ih_hi)):
                        pe.matmul(first_gi_ps[j][:, 0:G3], a[:, k, :], chunk(w, k, j), start=(k == 0 and a is xt_hi),
                                  stop=False)
                pe.wait_ge(w_lo_ready, k + 1)
                for j in range(NJ):
                    mm = pe.matmul(first_gi_ps[j][:, 0:G3], xt_hi[:, k, :], chunk(w_ih_lo, k, j), start=False,
                                   stop=(k == NJ - 1))
                    if k == NJ - 1:
                        mm.then_inc(gi_done, 1)
            pe.wait_ge(made, 6 + 1 + 2 * NJ)
            gi_chunk(Q, Q, 1)
            for s in range(S):
                step(0, s, first=True)
            with pe.Fori(1, NB - 1) as i:
                for s in range(S):
                    step(i, s)
            for s in range(S):
                step(NB - 1, s, last=True)

            pe.wait_ge(score_ready, 1)
            pe.matmul(fourth_ps[:, 0:NB], same_b[:], score_n[:].rearrange("p h n -> p (h n)"),
                      start=True, stop=True).then_inc(scores_ps_ready, 1)

            def recurrence_layout(dst, stationary, w, ks=range(NJ)):
                for k in ks:
                    for j in range(NJ):
                        mm = pe.matmul(dst[j * B:(j + 1) * B, 0:P], stationary[:, k * B:(k + 1) * B],
                                       w[:, k, j * P:(j + 1) * P], start=(k == 0), stop=(k == NJ - 1))
                return mm

            for _ in range(12):
                pe.matmul(third_ps[:, 0:G3], xt_hi[:, 0, :], w_ih_hi[:, 0, 0:G3], start=True, stop=True)
            pe.wait_ge(turned_ready, NB)
            recurrence_layout(keys_ps, br_turned, wk_t).then_inc(last_keys_ready, 1)
            pe.wait_ge(wo_centred, 2)
            recurrence_layout(gates_ps, br_turned, wo_t, (0, 1))
            quad_mean(NQ - 1)
            pe.wait_ge(last_dot_ready, 1)
            pe.wait_ge(last_sq_ready, 1)
            pe.matmul(third_ps[:, 0:2], same_b[:], last_key, start=True, stop=True).then_inc(last_sums_ready, 1)
            recurrence_layout(gates_ps, br_turned, wo_t, (2, 3)).then_inc(last_proj_ready, 1)
            pe.wait_ge(att_t_ready, 1)
            recurrence_layout(gi_ps[0], att_t, wo_t).then_inc(first_proj_ready, 1)

            def add_cp(c, number):
                bank, first_step = u_ps[c][number], c * C + number * Q
                pe.matmul(bank[:], ident[:], cx_all[:, first_step:first_step + Q, :], start=True, stop=False)
                pe.matmul(bank[:], ident[:], over_steps(cp), start=False, stop=True).then_inc(u_pe, 1)

            def spread_var(c):
                pe.wait_ge(act_squared, c + 1)
                if c < 2:
                    pe.wait_ge(dve_squared, (c + 1) * DVE_SHARE)
                wait(pe, var_ready, c)
                pe.matmul(small_ps[:, c * C:(c + 1) * C], same_b[:], sumsq[:, c * C:(c + 1) * C], start=True, stop=True
                          ).then_inc(var_summed, 1)

            pe.wait_ge(cx_ready, NQ)
            pe.wait_ge(cp_ready, 1)
            add_cp(2, 0)
            add_cp(2, 1)
            spread_var(0)
            add_cp(3, 0)
            spread_var(1)
            for number in range(1, Q):
                add_cp(3, number)
            spread_var(2)
            spread_var(3)

        @block.vector
        def _(dve):
            def split_x(quad):
                wait(dve, x_hi_ready, quad + 1)
                dve.tensor_tensor(xt_lo[:], x_t[:], xt_hi[:].bitcast(F32), ALU.subtract).then_inc(x_lo_ready, 1)

            def keep_gi(idx, pos):
                tok, j = pos % 2, pos % Q
                first = isinstance(idx, int) and idx < Q
                bank, dst = (first_gi_ps[j], first_tok[:, j, :]) if first else (gi_ps[tok], gi_tok[:, tok, :])
                wait(dve, gi_done, idx + 1)
                if not first:
                    wait(dve, gi_moved[tok], (idx - tok - Q) * 8)
                dve.tensor_tensor(dst.rearrange("p (g u) -> p g u", g=3),
                                  bank[:, 0:G3].rearrange("p (g u) -> p g u", g=3),
                                  b_in[:].rearrange("p (g j u) -> p j g u", g=3, j=NJ)[:, j],
                                  ALU.add).then_inc(gi_tok_ready, 1)

            parts = (slice(0, B), slice(B, 2 * B), slice(2 * B, P))
            first, rest = parts[0], slice(B, P)

            def take_n(number):
                c = parts[number]
                dve.scalar_tensor_tensor(out=n[:, c], in0=z[:, c], scalar=1.0, in1=n[:, c],
                                         op0=ALU.subtract, op1=ALU.mult).then_inc(terms_ready, 1)

            def add_terms(t, s, number):
                wait(dve, terms_ready, t * 5 + 3 + number)
                c = parts[number]
                dve.tensor_tensor(hist[:, s, c], zh[:, c], n[:, c], ALU.subtract).then_inc(h_ready, 1)

            def turn_state(t, s, number):
                wait(dve, h_ready, t * 3 + 1 + number)
                c = parts[number]
                dve.transpose(h_t[:, c], hist[:, s, c]).then_inc(ht_ready, 1)

            def quad_sum(slot, quad):
                wait(dve, x_res_ready, (quad + 1) * 16)
                wait(dve, xb_ready, quad)
                wait(dve, h_ready, quad * (3 * Q) + 3 * Q)
                dve.tensor_tensor(x1[:], hist[:, Q * slot:Q * slot + Q, :], x1[:], ALU.add
                                  ).then_inc(x1_ready, 1)

            def quad_partial_sums(quad):
                wait(dve, x1_ready, quad + 1)
                dve.tensor_reduce(sums[:], x1[:], AX.X, ALU.add).then_inc(sums_ready, 1)

            def quad_centre(quad):
                wait(dve, mean_ready, quad + 1)
                dve.scalar_tensor_tensor(out=cx_all[:, bass.ds(quad * Q, Q), :],
                                         in0=small_ps[:, 0:Q, None].broadcast_to([P, Q, P]),
                                         scalar=-1.0 / D, in1=x1[:], op0=ALU.mult, op1=ALU.add
                                         ).then_inc(cx_ready, 1)

            def quad_steps_sum(slot):
                dve.tensor_reduce(bs[:, slot, :], x1[:].rearrange("p t u -> p u t"), AX.X, ALU.add
                                  ).then_inc(bs_ready, 1)

            def block_sum(nb):
                wait(dve, bs_ready, nb * 2 + 2)
                dve.tensor_tensor(br_cur[:], bs[:, 0, :], bs[:, 1, :], ALU.add).then_inc(br_ready, 1)
                wait(dve, br_ready, nb + 1)
                dve.transpose(br_turned[:], br_cur[:]).then_inc(turned_ready, 1)

            def keys_dot(group):
                rows = slice(0, (4 - group) * B)
                dve.wait_ge(key_sq_ready, group + 1)
                wait(dve, key_dot_ready, group)
                dve.tensor_tensor_reduce(keys_wq[rows, :], gi_ps[group][rows, :], wq[rows, :], 1.0, 0.0, ALU.mult,
                                         ALU.add, key_dot[rows, group:group + 1]).then_inc(key_dot_ready, 1)

            def sum_ahead():
                dve.wait_ge(x_res_ready, NQ * 16)
                dve.tensor_reduce(bs[:, 1, :], x1[:].rearrange("p t u -> p u t"), AX.X, ALU.add).then_inc(pre_step, 1)
                dve.wait_ge(h_ready, 3 * T - 3)
                dve.tensor_reduce(h_sum[:], hist[:, Q:S - 1, :].rearrange("p t u -> p u t"), AX.X, ALU.add
                                  ).then_inc(pre_step, 1)
                keys_dot(1)
                dve.wait_ge(pre_step, 2)
                dve.tensor_tensor(bs[:, 1, :], bs[:, 1, :], h_sum[:], ALU.add).then_inc(pre_step, 1)
                dve.tensor_scalar(key_ss[:], key_ss[:], 1.0 / D, EPS, ALU.mult, ALU.add).then_inc(key_var_ready, 1)
                dve.wait_ge(pre_step, 3)
                dve.tensor_tensor(bs[:, 1, :], bs[:, 1, :], bs[:, 0, :], ALU.add).then_inc(pre_step, 1)
                dve.wait_ge(br_saved, NB - 1)
                dve.wait_ge(pre_step, 4)

            def score_keys():
                dve.wait_ge(key_rms_ready, 1)
                dve.wait_ge(key_dot_ready, 2)
                dve.tensor_tensor(score[:], key_dot[:], key_rms[:], ALU.mult).then_inc(key_dot_ready, 1)
                dve.wait_ge(key_dot_ready, 3)
                dve.tensor_tensor(score_n[:], score[:, :, None].broadcast_to([P, 2, NJ]),
                                  own_n[:, None, :].broadcast_to([P, 2, NJ]), ALU.mult).then_inc(score_ready, 1)

            def step(i, s, peeled=False, last=False):
                t = i * S + s
                slot, tt = s // Q, s % Q
                quad = i * 2 + slot
                wait(dve, rz_ready, t + 1)
                dve.tensor_tensor(r, gates_ps[:, 2 * P:G3], r, ALU.mult).then_inc(rh_ready, 1)
                before = hist[:, (s - 1) % S, :]
                dve.tensor_tensor(zh[:, first], z[:, first], before[:, first], ALU.mult).then_inc(terms_ready, 1)
                wait(dve, rh_ready, t + 1)
                for number, c in enumerate((first, rest)):
                    dve.tensor_tensor(n[:, c], r[:, c], gi[:, slot, tt * G3 + 2 * P:(tt + 1) * G3][:, c], ALU.add
                                      ).then_inc(n_pre_ready[number], 1)
                dve.tensor_tensor(zh[:, rest], z[:, rest], before[:, rest], ALU.mult).then_inc(terms_ready, 1)
                turned = not (last and s == S - 1)
                wait(dve, n_ready, t * 2 + 1)
                take_n(0)
                add_terms(t, s, 0)
                if turned:
                    turn_state(t, s, 0)
                wait(dve, n_ready, t * 2 + 2)
                take_n(1)
                take_n(2)
                add_terms(t, s, 1)
                add_terms(t, s, 2)
                if not turned:
                    return
                turn_state(t, s, 1)
                turn_state(t, s, 2)
                if not (last and t + 5 >= T):
                    keep_gi(t + 5, s + 5)
                if tt == 2 and not last:
                    split_x(quad + 2)
                if peeled and s < 3:
                    return
                done = (s + 1) // Q - 1
                dslot, dquad = done % 2, i * 2 + done
                if (s + 1) % Q == 0:
                    quad_sum(dslot, dquad)
                    quad_partial_sums(dquad)
                if (s + 1) % Q == 1:
                    quad_centre(dquad)
                if (s + 1) % Q == 2:
                    quad_steps_sum(dslot)
                if (s + 1) % Q == 3 and dslot == 1:
                    block_sum(i - 1)
                if last and s == 4:
                    keys_dot(0)
                if last and s == 6:
                    sum_ahead()
                    score_keys()

            def split_w(k):
                dve.wait_ge(w_hi_ready, k + 1)
                dve.tensor_tensor(w_ih_lo[:, k, :], w_stage[:, k, :], w_ih_hi[:, k, :].bitcast(F32),
                                  ALU.subtract).then_inc(w_lo_ready, 1)

            split_x(0)
            for k in range(NJ):
                split_w(k)
            dve.wait_ge(b_in_ready, 3)
            dve.wait_ge(h0_in, 16)
            for c in parts:
                dve.transpose(h_t[:, c], hist[:, S - 1, c]).then_inc(ht_ready, 1)
            for idx in range(Q):
                keep_gi(idx, idx)
            split_x(1)
            keep_gi(Q, Q)

            for s in range(S):
                step(0, s, peeled=True)
                if s == 2:
                    dve.wait_ge(consts_in, 16 * 6)
                    dve.tensor_tensor(wq[:], wq[:], q_row, ALU.mult).then_inc(wq_ready, 1)
                    dve.tensor_tensor(wq_rec[:], wq_rec[:], q_row_rec, ALU.mult).then_inc(wq_ready, 1)
                if s in (4, 5):
                    dve.wait_ge(wo_in, 16)
                    ks = slice((s - 4) * 2, (s - 4) * 2 + 2)
                    dve.tensor_reduce(wo_sum[:, ks], wo_t[:, ks, :], AX.X, ALU.add).then_inc(wo_summed, 1)
                if s in (6, 7):
                    dve.wait_ge(wo_summed, 2)
                    ks = slice((s - 6) * 2, (s - 6) * 2 + 2)
                    dve.scalar_tensor_tensor(out=wo_t[:, ks, :], in0=wo_sum[:, ks, None].broadcast_to([P, 2, D]),
                                             scalar=-1.0 / D, in1=wo_t[:, ks, :], op0=ALU.mult, op1=ALU.add
                                             ).then_inc(wo_centred, 1)
            with dve.Fori(1, NB - 1) as i:
                for s in range(S):
                    step(i, s)
            for s in range(S):
                step(NB - 1, s, last=True)

            dve.wait_ge(h_ready, 3 * T)
            dve.tensor_tensor(br_cur[:], bs[:, 1, :], hist[:, S - 1, :], ALU.add).then_inc(br_ready, 1)
            dve.wait_ge(br_ready, NB)
            dve.transpose(br_turned[:], br_cur[:]).then_inc(turned_ready, 1)
            dve.wait_ge(scores_ps_ready, 1)
            dve.tensor_reduce(top[:, 0:1], fourth_ps[:, 0:NB - 1], AX.X, ALU.max).then_inc(top_step, 1)
            dve.tensor_reduce(neg_max, fourth_ps[:, 0:NB - 1], AX.X, ALU.max, negate=True).then_inc(max_ready, 1)
            quad_sum(1, NQ - 1)
            dve.wait_ge(probs_ready, 1)
            dve.tensor_tensor(att_w, br_all[:, 0:(NB - 1) * P].rearrange("p (n u) -> p n u", u=P),
                              probs[:, :, None].broadcast_to([P, NB - 1, P]), ALU.mult).then_inc(att_step, 1)
            dve.wait_ge(wq_ready, 2)
            dve.wait_ge(last_keys_ready, 1)
            dve.tensor_tensor_reduce(keys_wq[:, 0:P], keys_ps[:, 0:P], wq_rec[:], 1.0, 0.0, ALU.mult, ALU.add,
                                     last_key[:, 1:2]).then_inc(last_dot_ready, 1)
            dve.wait_ge(att_step, 1)
            dve.tensor_reduce(att_first, att_w.rearrange("p n u -> p u n"), AX.X, ALU.add).then_inc(att_step, 1)
            dve.wait_ge(last_sums_ready, 1)
            dve.tensor_scalar(last_var, third_ps[:, 0:1], 1.0 / D, EPS, ALU.mult, ALU.add
                              ).then_inc(last_var_ready, 1)
            dve.wait_ge(att_step, 2)
            dve.transpose(att_t, att_first).then_inc(att_t_ready, 1)
            quad_centre(NQ - 1)
            dve.wait_ge(last_rms_ready, 1)
            dve.tensor_tensor(top[:, 1:2], third_ps[:, 1:2], last_rms, ALU.mult).then_inc(top_step, 1)
            dve.wait_ge(top_step, 2)
            dve.tensor_reduce(top_max, top, AX.X, ALU.max).then_inc(top_step, 1)
            dve.wait_ge(top_step, 3)
            dve.tensor_scalar(top, top, top_max[:, 0:1], None, ALU.subtract).then_inc(top_step, 1)
            dve.wait_ge(share_ready, 1)
            dve.wait_ge(last_proj_ready, 1)
            dve.tensor_scalar(cp, gates_ps[:, 0:P], share[:, 1:2], None, ALU.mult).then_inc(cp_step, 1)
            dve.scalar_tensor_tensor(out=denom, in0=prob_sum, scalar=share[:, 0:1], in1=share[:, 1:2],
                                     op0=ALU.mult, op1=ALU.add).then_inc(denom_step, 1)
            dve.wait_ge(first_proj_ready, 1)
            dve.wait_ge(cp_step, 1)
            dve.scalar_tensor_tensor(out=cp, in0=gi_ps[0][:, 0:P], scalar=share[:, 0:1], in1=cp,
                                     op0=ALU.mult, op1=ALU.add).then_inc(cp_step, 1)
            dve.wait_ge(denom_step, 1)
            dve.reciprocal(denom, denom).then_inc(denom_step, 1)
            dve.wait_ge(cp_step, 2)
            dve.wait_ge(denom_step, 2)
            dve.tensor_scalar(cp, cp, denom[:, 0:1], None, ALU.mult).then_inc(cp_ready, 1)

            def dve_square(c, first, end_):
                dve.wait_ge(*u_count(c, end_ - 1))
                for t in range(first, end_):
                    dve.tensor_tensor_reduce(dve_squares[:, c * DVE_SHARE + t - DVE_SQUARES[c][0], :], u_of(c, t),
                                             u_of(c, t), 1.0, 0.0, ALU.mult, ALU.add,
                                             sumsq[:, c * C + t:c * C + t + 1]).then_inc(dve_squared, 1)

            def refine(c, part):
                steps = slice(c * C, (c + 1) * C)
                v, r, f = var[:, steps], rstd[:, steps], fix[:, steps]
                if part == 0:
                    dve.wait_ge(var_summed, c + 1)
                    dve.tensor_scalar(v, small_ps[:, steps], 1.0 / D, EPS, ALU.mult, ALU.add).then_inc(var_ready, 1)
                    return
                if part == 1:
                    dve.wait_ge(dev_ready, c + 1)
                    ins = dve.reciprocal(r, dev[:, steps])
                else:
                    dve.wait_ge(refine_step, 5 * c + part - 1)
                    if part == 2:
                        ins = dve.tensor_tensor(f, v, r, ALU.mult)
                    if part == 3:
                        ins = dve.tensor_tensor(f, f, r, ALU.mult)
                    if part == 4:
                        ins = dve.tensor_scalar(f, f, -0.5, 1.5, ALU.mult, ALU.add)
                    if part == 5:
                        ins = dve.tensor_tensor(r, r, f, ALU.mult)
                ins.then_inc(refine_step, 1)

            def scale(c):
                dve.wait_ge(refine_step, 5 * c + 5)
                for t in range(C if c < 2 else S):
                    ins = dve.scalar_tensor_tensor(out=cx_all[:, c * C + t, :], in0=u_of(c, t),
                                                   scalar=rstd[:, c * C + t:c * C + t + 1], in1=gamma[:],
                                                   op0=ALU.mult, op1=ALU.mult)
                    if t % S == S - 1:
                        ins.then_inc(scaled, 1)
                    if c < 2 and t == 7:
                        refine(c + 1, 0)
                    if c < 2 and t > 10:
                        refine(c + 1, t - 10)
                    if c == 2 and t == 5:
                        refine(3, 0)

            def times_gamma(first_step, number):
                dve.wait_ge(act_scaled, number)
                v = cx_all[:, first_step:first_step + Q, :]
                return dve.tensor_tensor(v, v, over_steps(gamma), ALU.mult)

            def add_cp(first):
                v = cx_all[:, first:first + Q, :]
                dve.tensor_tensor(v, v, over_steps(cp), ALU.add).then_inc(u_dve, 1)

            dve.wait_ge(cp_ready, 1)
            for first in range(0, C, Q):
                add_cp(first)
            dve_square(0, *DVE_SQUARES[0])
            dve_square(1, 0, DVE_SHARE // 2)
            refine(0, 0)
            dve_square(1, DVE_SHARE // 2, DVE_SHARE)
            for part in range(1, 6):
                refine(0, part)
            for c in range(3):
                scale(c)
            refine(3, 1)
            times_gamma(2 * C + S, 1)
            refine(3, 2)
            refine(3, 3)
            times_gamma(2 * C + S + Q, 2).then_inc(scaled, 1)
            refine(3, 4)
            refine(3, 5)
            scale(3)
            dve.wait_ge(xb_ready, NQ)
            for number, first_step in enumerate((T - S, T - Q)):
                steps = slice(first_step, first_step + Q)
                v = cx_all[:, steps, :]
                times_gamma(first_step, number + 3).then_inc(scaled, 1)
                dve.wait_ge(scaled, NB + number)
                dve.tensor_tensor(v, v, xb_all[:, steps, :], ALU.add).then_inc(out_dve, 1)


def kernel(**inputs):
    import numpy as _np
    import concourse.bacc as _bacc
    from concourse import mybir as _mybir
    from concourse.bass_utils import run_bass_kernel_spmd as _run

    nc = _bacc.Bacc("TRN2", target_bir_lowering=False, num_devices=1)
    x, cond = inputs["x"], inputs["cond_2048"]
    laid_out = {
        "x_rec": x.reshape(B, T, NJ, P).transpose(2, 0, 1, 3).reshape(P, T, P),
        "x_t": x.reshape(B, NQ, Q, NJ, P).transpose(4, 1, 3, 0, 2).reshape(P, NQ * NJ, P),
        "cond": cond.reshape(B, NJ, P).transpose(1, 0, 2).reshape(P, P),
        "w_ih": inputs["L0_cond_W_ih"], "w_hh": inputs["L0_cond_W_hh"],
        "b_ih": inputs["L0_cond_b_ih"], "b_hh": inputs["L0_cond_b_hh"], "rms_weight": inputs["L1_cond_rms_weight"],
        "wk_t": inputs["L1_cond_Wk"].transpose(1, 0), "wo_t": inputs["L1_cond_Wo"].transpose(1, 0),
        "gamma": inputs["L1_cond_ln_gamma"], "beta": inputs["L1_cond_ln_beta"],
    }
    for name in ("w_hh", "wk_t", "wo_t"):
        w = laid_out[name]
        laid_out[name] = w.reshape(NJ, NJ, B, w.shape[1]).transpose(1, 0, 2, 3).reshape(w.shape)
    arrays, args = {}, []
    for name, a in laid_out.items():
        a = _np.ascontiguousarray(a)
        arrays[f"in_{name}_dram"] = a
        args.append(nc.dram_tensor(f"in_{name}_dram", a.shape, _mybir.dt.from_np(a.dtype), kind="ExternalInput").ap())
    args.append(nc.dram_tensor("out_dram", (P, T, P), F32, kind="ExternalOutput").ap())
    gru_block_attention(nc, *args)
    r = _run(nc, [arrays], core_ids=[0])
    got = r.results[0]["out_dram"].reshape(NJ, B, T, P)
    return _np.ascontiguousarray(got.transpose(1, 2, 0, 3)).reshape(B, T, D)
```
